# Optimizing a Trainium2 kernel written in Bass

```python
import numpy as np
import jax
import jax.numpy as jnp

def _softmax(x, axis=-1):
    return jax.nn.softmax(x, axis=axis)

def _gelu(x):
    return jax.nn.gelu(x, approximate=True)

def _silu(x):
    return jax.nn.silu(x)

def _sigmoid(x):
    return jax.nn.sigmoid(x)

def _layernorm(x, axis=-1, eps=1e-05):
    m = jnp.mean(x, axis=axis, keepdims=True)
    v = jnp.var(x, axis=axis, keepdims=True)
    return (x - m) / jnp.sqrt(v + eps)

def _scatter_add(tgt, idx, src, axis=0):
    return tgt.at[idx].add(src)

def _segment_sum(src, seg, n):
    return jax.ops.segment_sum(src, seg, n)
kernel_name = 'mk_prb_d1_jaxref_r8_4a0a99'

def setup_inputs(seed: int=0):
    np.random.seed(seed)
    _w = jnp.asarray

    def _L0_attn_setup():
        import jax, jax.numpy as jnp
        import numpy as np
        import math
        B, T, D = (4, 512, 128)
        H, DK, DV, C = (8, 128, 128, 64)

        def _rms_norm(x, eps=1e-06):
            return x * jax.lax.rsqrt(jnp.mean(x * x, axis=-1, keepdims=True) + eps)
        key = jax.random.key(seed)
        ks = jax.random.split(key, 7)
        s = 0.02
        return {'x': jax.random.normal(ks[0], (B, T, D), jnp.float32), 'Wq': jax.random.normal(ks[1], (H * DK, D), jnp.float32) * s, 'Wk': jax.random.normal(ks[2], (H * DK, D), jnp.float32) * s, 'Wv': jax.random.normal(ks[3], (H * DV, D), jnp.float32) * s, 'Wg': jax.random.normal(ks[4], (H, D), jnp.float32) * s, 'bg': jnp.full((H,), 3.0, jnp.float32), 'Wo': jax.random.normal(ks[5], (D, H * DV), jnp.float32) * s, 'qk_gain': jnp.asarray(4.0, jnp.float32)}
    _L0_attn_in = _L0_attn_setup()

    def _L0_ffn_setup():
        import jax, jax.numpy as jnp
        import numpy as np
        N, T, D = (4, 512, 128)
        NUM_EXPERTS = 8
        EXPERT_CAP = 2.0
        MLP_RATIO = 4
        HIDDEN = MLP_RATIO * D
        key = jax.random.key(seed)
        k1, k2, k3, k4 = jax.random.split(key, 4)
        x = jax.random.normal(k1, (N, T, D), dtype=jnp.float32)
        gate_w = jax.random.truncated_normal(k2, -2.0, 2.0, (D, NUM_EXPERTS), dtype=jnp.float32) * 0.02
        w1 = jax.random.normal(k3, (NUM_EXPERTS, D, HIDDEN), dtype=jnp.float32) * 0.02
        w2 = jax.random.normal(k4, (NUM_EXPERTS, HIDDEN, D), dtype=jnp.float32) * 0.02
        return {'x': x, 'gate_w': gate_w, 'w1': w1, 'w2': w2}
    _L0_ffn_in = _L0_ffn_setup()
    _d = {'L0_attn_x': _L0_attn_in['x'], 'L0_attn_Wq': _L0_attn_in['Wq'], 'L0_attn_Wk': _L0_attn_in['Wk'], 'L0_attn_Wv': _L0_attn_in['Wv'], 'L0_attn_Wg': _L0_attn_in['Wg'], 'L0_attn_bg': _L0_attn_in['bg'], 'L0_attn_Wo': _L0_attn_in['Wo'], 'L0_attn_qk_gain': _L0_attn_in['qk_gain'], 'L0_ffn_gate_w': _L0_ffn_in['gate_w'], 'L0_ffn_w1': _L0_ffn_in['w1'], 'L0_ffn_w2': _L0_ffn_in['w2']}
    _x0 = _d['L0_attn_x']
    _d['L0_attn_x'] = jax.random.normal(jax.random.fold_in(jax.random.key(seed), 1), (8, 256, 128), dtype=_x0.dtype)
    del _x0
    return _d

def reference(L0_attn_x, L0_attn_Wq, L0_attn_Wk, L0_attn_Wv, L0_attn_Wg, L0_attn_bg, L0_attn_Wo, L0_attn_qk_gain, L0_ffn_gate_w, L0_ffn_w1, L0_ffn_w2):

    def _L0_attn_ref(x, Wq, Wk, Wv, Wg, bg, Wo, qk_gain):
        import jax, jax.numpy as jnp
        import numpy as np
        import math
        B, T, D = (4, 512, 128)
        H, DK, DV, C = (8, 128, 128, 64)

        def _rms_norm(x, eps=1e-06):
            return x * jax.lax.rsqrt(jnp.mean(x * x, axis=-1, keepdims=True) + eps)
        Bs, Ts, Ds = x.shape
        pad = (C - Ts % C) % C
        if pad:
            x = jnp.pad(x, ((0, 0), (0, pad), (0, 0)))
        Tp = x.shape[1]
        n = Tp // C
        q = (x @ Wq.T).reshape(Bs, Tp, H, DK).transpose(0, 2, 1, 3)
        k = (x @ Wk.T).reshape(Bs, Tp, H, DK).transpose(0, 2, 1, 3)
        v = (x @ Wv.T).reshape(Bs, Tp, H, DV).transpose(0, 2, 1, 3)
        g = jax.nn.sigmoid(x @ Wg.T + bg).transpose(0, 2, 1)
        q = _rms_norm(q) * qk_gain
        k = _rms_norm(k)
        q = q.reshape(Bs, H, n, C, DK)
        k = k.reshape(Bs, H, n, C, DK)
        v = v.reshape(Bs, H, n, C, DV)
        g = g.reshape(Bs, H, n, C)
        mask = jnp.tril(jnp.ones((C, C), bool))
        scores = jnp.einsum('bhntd,bhnsd->bhnts', q, k) / math.sqrt(DK)
        scores = jnp.where(mask, scores, -jnp.inf)
        attn = jax.nn.softmax(scores, axis=-1)
        y_in = jnp.einsum('bhnts,bhnsd->bhntd', attn, v)
        kv = jnp.einsum('bhntd,bhnte->bhnde', k, v)
        gamma = jnp.exp(jnp.sum(jnp.log(g), axis=-1))
        qs = jnp.moveaxis(q, 2, 0)
        kvs = jnp.moveaxis(kv, 2, 0)
        gs = jnp.moveaxis(gamma, 2, 0)

        def step(state, inp):
            qn, kvn, gn = inp
            yc = jnp.einsum('bhtd,bhde->bhte', qn, state)
            new_state = state * gn[:, :, None, None] + kvn
            return (new_state, yc)
        state0 = jnp.zeros((Bs, H, DK, DV), x.dtype)
        _, ycs = jax.lax.scan(step, state0, (qs, kvs, gs))
        y_cross = jnp.moveaxis(ycs, 0, 2)
        y = (y_in + y_cross).reshape(Bs, H, Tp, DV).transpose(0, 2, 1, 3).reshape(Bs, Tp, H * DV)
        y = y @ Wo.T
        if pad:
            y = y[:, :Ts, :]
        return y

    def _L0_ffn_ref(x, gate_w, w1, w2):
        import jax, jax.numpy as jnp
        import numpy as np
        N, T, D = (4, 512, 128)
        NUM_EXPERTS = 8
        EXPERT_CAP = 2.0
        MLP_RATIO = 4
        HIDDEN = MLP_RATIO * D
        x = x.astype(jnp.float32)
        n, t, d = x.shape
        k = int(EXPERT_CAP * t / NUM_EXPERTS)
        scores = jnp.einsum('ntd,de->nte', x, gate_w)
        probs = jax.nn.softmax(scores, axis=-1)
        probs = jnp.transpose(probs, (0, 2, 1))
        g, m = jax.lax.top_k(probs, k)
        xin = jax.vmap(lambda xb, mb: xb[mb])(x, m)
        h = jax.nn.gelu(jnp.einsum('nekd,edf->nekf', xin, w1))
        h = jnp.einsum('nekf,efd->nekd', h, w2)
        weighted = g[..., None] * h
        flat_idx = (m + jnp.arange(n, dtype=m.dtype)[:, None, None] * t).reshape(-1)
        out = jnp.zeros((n * t, d), dtype=jnp.float32).at[flat_idx].add(weighted.reshape(-1, d))
        out = out.reshape(n, t, d)
        return out.astype(jnp.bfloat16)
    x = L0_attn_x
    xn = _layernorm(x, axis=-1)
    x = x + _L0_attn_ref(xn, L0_attn_Wq, L0_attn_Wk, L0_attn_Wv, L0_attn_Wg, L0_attn_bg, L0_attn_Wo, L0_attn_qk_gain) + _L0_ffn_ref(xn, L0_ffn_gate_w, L0_ffn_w1, L0_ffn_w2)
    return x

_drawn_inputs = setup_inputs


def setup_inputs(seed=0):
    import zlib

    import numpy as np

    out = dict(_drawn_inputs(seed))
    spreads = {'L0_attn_bg': (3.0, 0.6)}
    factors = {'L0_attn_Wg': 35.011, 'L0_ffn_gate_w': 8.0, 'L0_ffn_w1': 8.0, 'L0_ffn_w2': 8.0}
    for name, (base, spread) in spreads.items():
        noise = np.random.default_rng([zlib.crc32(name.encode()), seed]).standard_normal(out[name].shape)
        drawn = base * np.exp(spread * noise) if base else spread * noise
        out[name] = jnp.asarray(drawn.astype(out[name].dtype))
    for name, factor in factors.items():
        out[name] = (out[name] * factor).astype(out[name].dtype)
    return out
```

```python
import math
import concourse.bass as bass
from concourse import mybir
from contextlib import ExitStack


def norm_attention_and_expert_choice_ffn_kernel(
    nc: bass.Bass,
    x: bass.AP,
    Wq: bass.AP,
    Wk: bass.AP,
    Wv: bass.AP,
    Wg: bass.AP,
    bg: bass.AP,
    Wo: bass.AP,
    qk_gain: bass.AP,
    gate_w: bass.AP,
    w1: bass.AP,
    w2: bass.AP,
    out: bass.AP,
):
    fp32 = mybir.dt.float32
    fp32r = mybir.dt.float32r
    fp16 = mybir.dt.float16
    bf16 = mybir.dt.bfloat16
    i32 = mybir.dt.int32
    u32 = mybir.dt.uint32
    ALU = mybir.AluOpType
    ACT = mybir.ActivationFunctionType
    AX = mybir.AxisListType
    ds = bass.ds

    P = 128
    B, T, D = x.shape
    HT = T // P
    NT = B * HT
    H = Wg.shape[0]
    C = 64
    G = 4
    GW = G * P
    E = gate_w.shape[1]
    F = w1.shape[2]
    FT = F // P
    K = 2 * T // E
    BP = B * K // P
    TOPS = 8
    LN_EPS, RMS_EPS = 1e-5, 1e-6
    NEG = -1.0e30
    UNIT = 2.0 * P
    assert D == P and HT == 2 and T == 4 * C and H == 2 * G and 2 * K == P and B * E == 64 and E == H

    def bc(ap, *shape):
        return ap.broadcast_to(list(shape))

    ctx = ExitStack()
    with ctx:
        def sb(name, shape, dt=fp32):
            return ctx.enter_context(nc.sbuf_tensor(name, shape, dt))

        def sem(name):
            return ctx.enter_context(nc.semaphore(name))

        def sems(name, n):
            return [sem(f"{name}{i}") for i in range(n)]

        bank = [ctx.enter_context(nc.psum_tensor(f"bank{i}", [P, 512], fp32)) for i in range(8)]

        x_in = sb("x_in", [P, NT, D])
        xn_h = sb("xn_h", [P, NT, D], fp16)
        xn_l = sb("xn_l", [P, NT, D], fp16)
        xT_all = sb("xT_all", [P, B, 2, T], fp32r)
        proj_w = sb("proj_w", [P, 3, 2, H * P], fp32r)
        decay = sb("decay", [P, B, H, 2])
        score_c = sb("score_c", [P, 1])
        cross_c = sb("cross_c", [P, 1])
        causal = sb("causal", [P, C])
        ident = sb("ident", [P, P])
        ident_b = sb("ident_b", [P, P], bf16)
        slot_gate = sb("slot_gate", [P, E, BP])
        slot_tok = sb("slot_tok", [P, E, BP])
        tok_spread = sb("tok_spread", [B * E, E * K], fp16)
        pick_b = sb("pick_b", [B * E, B, P], fp16)
        tok_col = sb("tok_col", [P, HT])
        tok_row = sb("tok_row", [P, HT * T])

        with ExitStack() as c1:
            def sb1(name, shape, dt=fp32):
                return c1.enter_context(nc.sbuf_tensor(name, shape, dt))

            def sem1(name):
                return c1.enter_context(nc.semaphore(name))

            wq_in = sb1("wq_in", [P, H, D])
            wk_in = sb1("wk_in", [P, H, D])
            wv_in = sb1("wv_in", [P, H, D])
            wo_in = sb1("wo_in", [P, H * P])
            wo_T = sb1("wo_T", [P, H, D])
            gates_w = sb1("gates_w", [P, H + E])
            bg_in = sb1("bg_in", [P, H])
            gain_in = sb1("gain_in", [P, 1])
            stats = sb1("stats", [P, NT, 6])
            mv = sb1("mv", [P, NT, 2])
            var = sb1("var", [P, NT])
            lnv = sb1("lnv", [P, NT])
            rs = sb1("rs", [P, NT])
            nw = sb1("nw", [P, NT])
            rstd = sb1("rstd", [P, NT])
            xn = sb1("xn", [P, NT, D])
            xT = sb1("xT", [P, NT * P])
            z = sb1("z", [P, NT, H])
            za = sb1("za", [P, NT, H])
            zn = sb1("zn", [P, NT, H])
            logg = sb1("logg", [P, NT, H])
            later = sb1("later", [P, P])
            whole = sb1("whole", [P, P])
            gmax = sb1("gmax", [P, NT])
            gsh = sb1("gsh", [P, NT, E])
            gsum = sb1("gsum", [P, NT])
            ginv = sb1("ginv", [P, NT])
            probs = sb1("probs", [P, HT, B, E])
            pT = [sb1(f"pT{i}", [B * E, T]) for i in range(2)]
            top = sb1("top", [B * E, 2, K])
            top_i = sb1("top_i", [B * E, K], u32)
            top_t = sb1("top_t", [B * E, 2, K])
            emask = sb1("emask", [B * E, E])
            bmask = sb1("bmask", [B * E, B])
            row_i = sb1("row_i", [P, HT * T], i32)
            col_i = sb1("col_i", [P, HT], i32)

            load_x = sem1("load_x")
            load_w = sem1("load_w")
            load_s = sem1("load_s")
            made = sem1("made")
            d = sem1("dve1")
            a = sem1("act1")
            pe_s = sem1("pe1")

            dve_at, act_at, pe_at = {}, {}, {}
            N_CONST = 20

            block = c1.enter_context(nc.Block())

            for n, name in enumerate(["woT0", "woT1", "q0", "q1", "k0", "k1", "xT0", "xT1", "xT2", "xT3", "logits",
                                      "n0", "n1", "decay", "probsT", "slots"]):
                pe_at[name] = n + 1
            for n, name in enumerate(["woT0", "woT1", "q0", "q1", "k0", "k1", "ln_v", "rs", "xT0", "xT1", "xT2", "xT3",
                                      "xh", "gexp", "zexp", "zln", "n0", "n1", "decay2", "decay3"]):
                act_at[name] = n + 1
            steps = ["zero"] + [f"st{t}" for t in range(NT)] + [f"mv{t}" for t in range(NT)]
            steps += ["var", "q0", "q1", "k0", "k1", "nw1", "nw2", "nw3", "rstd"] + [f"xn{t}" for t in range(NT)]
            steps += ["xTh0", "xTl0", "xTh1", "xTl1", "xTh2", "xTl2", "xTh3", "xTl3"]
            steps += ["gmax", "gsh", "z", "zn", "za", "gsum", "ginv", "probs", "logg", "xl", "cross_c", "score_c", "pT"]
            for r in range(K // TOPS):
                steps += [f"top{r}", f"idx{r}"] + ([f"cut{r}"] if r < K // TOPS - 1 else [])
            steps += ["n0", "n1", "decay", "top_copy", "tokf", "tokf2", "emask", "bmask", "spread", "pick",
                      "gate0", "gate1", "tok0", "tok1", "tok_row", "tok_col"]
            for n, name in enumerate(steps):
                dve_at[name] = n + 1

            @block.sync
            def _(sp):
                sp.dma_start(x_in[:, :, :], x.rearrange("b (h p) d -> p (b h) d", p=P)).then_inc(load_x, 16)
                sp.dma_start(wo_in[:, :], Wo).then_inc(load_w, 16)
                sp.dma_start(wk_in[:, :, :], Wk.rearrange("(h p) d -> p h d", p=P)).then_inc(load_w, 16)
                sp.wait_ge(load_x, 16)
                sp.wait_ge(load_w, 64)
                sp.wait_ge(load_s, 64)

            @block.gpsimd
            def _(pool):
                n = 0

                def done(ins):
                    nonlocal n
                    n += 1
                    ins.then_inc(made, 1)
                    pool.wait_ge(made, n)

                done(pool.memset(ident[:, :], 0.0))
                done(pool.memset(causal[:, :], 0.0))
                done(pool.affine_select(out=ident[:, :], in_=ident[:, :], compare_op=ALU.not_equal, fill=1.0, base=0,
                                        pattern=[[-1, P]], channel_multiplier=1))
                for c in range(2):
                    rows = causal[c * C:(c + 1) * C, :]
                    done(pool.affine_select(out=rows, in_=rows, compare_op=ALU.is_ge, fill=NEG, base=0,
                                            pattern=[[-1, C]], channel_multiplier=1))
                done(pool.memset(later[:, :], 0.0))
                done(pool.memset(whole[:, :], 0.0))
                done(pool.memset(later[C:P, 0:C], 1.0))
                done(pool.memset(whole[0:C, :], 1.0))
                done(pool.tensor_copy(ident_b[:, :], ident[:, :]))
                done(pool.iota(row_i[:, :], pattern=[[1, HT * T]], base=0, channel_multiplier=0))
                done(pool.iota(col_i[:, :], pattern=[[P, HT]], base=0, channel_multiplier=1))
                assert n == 12

            @block.scalar
            def _(act):
                act.dma_start(wv_in[:, :, :], Wv.rearrange("(h p) d -> p h d", p=P)).then_inc(load_w, 16)
                act.dma_start(wq_in[:, :, :], Wq.rearrange("(h p) d -> p h d", p=P)).then_inc(load_w, 16)
                act.dma_start(gates_w[:, H:H + E], gate_w).then_inc(load_s, 16)
                act.dma_start(gates_w[:, 0:H], Wg.rearrange("h d -> d h"), allow_slow_non_contiguous=True)\
                   .then_inc(load_s, 16)
                act.dma_start(bg_in[:, :], bg.partition_broadcast(P)).then_inc(load_s, 16)
                act.dma_start(gain_in[:, :], qk_gain.partition_broadcast(P)).then_inc(load_s, 16)
                n = 0

                def done(name, ins):
                    nonlocal n
                    n += 1
                    assert act_at[name] == n, name
                    ins.then_inc(a, 1)

                for j in range(2):
                    act.wait_ge(pe_s, pe_at[f"woT{j}"])
                    done(f"woT{j}", act.activation(wo_T[:, G * j:G * (j + 1), :].rearrange("p h d -> p (h d)"),
                                                   bank[j][:, :], ACT.Copy))
                for w, name in enumerate("qk"):
                    for j in range(2):
                        act.wait_ge(pe_s, pe_at[f"{name}{j}"])
                        done(f"{name}{j}", act.activation(proj_w[:, w, 0, j * GW:(j + 1) * GW],
                                                          bank[2 + 2 * w + j][:, :], ACT.Copy))
                act.wait_ge(d, dve_at["var"])
                done("ln_v", act.activation(lnv[:, :], var[:, :], ACT.Ln))
                act.wait_ge(a, act_at["ln_v"])
                done("rs", act.activation(rs[:, :], lnv[:, :], ACT.Exp, scale=-0.5))
                for m in range(4):
                    act.wait_ge(pe_s, pe_at[f"xT{m}"])
                    done(f"xT{m}", act.activation(xT[:, m * 512:(m + 1) * 512], bank[(6 + m) % 8][:, :], ACT.Copy))
                act.wait_ge(d, dve_at[f"xn{NT - 1}"])
                done("xh", act.activation(xn_h[:, :, :], xn[:, :, :], ACT.Copy))
                act.wait_ge(d, dve_at["gsh"])
                done("gexp", act.activation(gsh[:, :, :], gsh[:, :, :], ACT.Exp))
                act.wait_ge(d, dve_at["za"])
                done("zexp", act.activation(za[:, :, :], za[:, :, :], ACT.Exp, scale=-1.0))
                act.wait_ge(a, act_at["zexp"])
                done("zln", act.activation(za[:, :, :], za[:, :, :], ACT.Ln, bias=1.0))
                for j in range(2):
                    act.wait_ge(pe_s, pe_at[f"n{j}"])
                    done(f"n{j}", act.activation(proj_w[:, 2, 0, j * GW:(j + 1) * GW], bank[3 + j][:, :], ACT.Copy))
                act.wait_ge(pe_s, pe_at["decay"])
                for k in range(2):
                    done(f"decay{2 + k}", act.activation(
                        decay[:, :, :, k].rearrange("p b h -> p (b h)"), bank[5][:, k * B * H:(k + 1) * B * H],
                        ACT.Exp, scale=-1.0))

            @block.tensor
            def _(pe):
                n = 0

                def done(name, ins):
                    nonlocal n
                    n += 1
                    assert pe_at[name] == n, name
                    ins.then_inc(pe_s, 1)

                pe.wait_ge(made, 3)
                pe.wait_ge(load_w, 64)
                for j in range(2):
                    for h in range(G):
                        mm = pe.transpose(bank[j][:, h * P:(h + 1) * P], wo_in[:, (G * j + h) * P:(G * j + h + 1) * P],
                                          ident[:, :])
                    done(f"woT{j}", mm)
                for w, (name, w_in) in enumerate((("q", wq_in), ("k", wk_in))):
                    for j in range(2):
                        for h in range(G):
                            mm = pe.transpose(bank[2 + 2 * w + j][:, h * P:(h + 1) * P], w_in[:, G * j + h, :],
                                              ident[:, :])
                        done(f"{name}{j}", mm)
                for m in range(4):
                    pe.wait_ge(d, dve_at[f"xn{4 * m + 3}"])
                    if m >= 2:
                        pe.wait_ge(a, act_at[f"woT{m - 2}"])
                    for t in range(4):
                        mm = pe.transpose(bank[(6 + m) % 8][:, t * P:(t + 1) * P], xn[:, 4 * m + t, :], ident[:, :])
                    done(f"xT{m}", mm)
                pe.wait_ge(load_s, 64)
                pe.wait_ge(d, dve_at["q1"])
                for t in range(NT):
                    pe.wait_ge(a, act_at[f"xT{t // 4}"])
                    mm = pe.matmul(bank[2][:, t * (H + E):(t + 1) * (H + E)], xT[:, t * P:(t + 1) * P], gates_w[:, :],
                                   start=True, stop=True)
                done("logits", mm)
                pe.wait_ge(d, dve_at["k1"])
                for j in range(2):
                    for h in range(G):
                        mm = pe.matmul(bank[3 + j][:, h * P:(h + 1) * P], wv_in[:, G * j + h, :], wo_T[:, G * j + h, :],
                                       start=True, stop=True)
                    done(f"n{j}", mm)
                pe.wait_ge(made, 9)
                pe.wait_ge(d, dve_at["logg"])
                by_tile = logg[:, :, :].rearrange("p (b t) h -> p t b h", t=HT)
                BH = B * H
                pe.matmul(bank[5][:, 0:BH], later[:, :], by_tile[:, 0], start=True, stop=True)
                pe.matmul(bank[5][:, BH:2 * BH], later[:, :], by_tile[:, 0], start=True, stop=False)
                done("decay", pe.matmul(bank[5][:, BH:2 * BH], whole[:, :], by_tile[:, 1], start=False, stop=True))
                for t in range(HT):
                    mm = pe.transpose(bank[6][0:B * E, t * P:(t + 1) * P],
                                      probs[:, t, :, :].rearrange("p b e -> p (b e)"), ident[:, :])
                done("probsT", mm)
                pe.wait_ge(d, dve_at["tokf2"])
                pe.transpose(bank[7][:, 0:B * E], top[:, :, :].rearrange("p a k -> p (a k)"), ident[0:B * E, 0:B * E])
                done("slots", pe.transpose(bank[7][:, 64:64 + B * E], top_t[:, :, :].rearrange("p a k -> p (a k)"),
                                           ident[0:B * E, 0:B * E]))

            @block.vector
            def _(dve):
                n = 0

                def done(name, ins):
                    nonlocal n
                    n += 1
                    assert dve_at[name] == n, (name, n)
                    ins.then_inc(d, 1)

                def after(name):
                    dve.wait_ge(d, dve_at[name])

                done("zero", dve.memset(mv[:, :, :], 0.0))
                dve.wait_ge(load_x, 16)
                for t in range(NT):
                    done(f"st{t}", dve.bn_stats(stats[:, t, :], x_in[:, t, :]))
                after(f"st{NT - 1}")
                for t in range(NT):
                    done(f"mv{t}", dve.bn_aggr(mv[:, t, :], stats[:, t, :]))
                after(f"mv{NT - 1}")
                done("var", dve.tensor_scalar(var[:, :], mv[:, :, 1], LN_EPS, None, ALU.add))
                for w, name in enumerate("qk"):
                    for j in range(2):
                        dve.wait_ge(a, act_at[f"{name}{j}"])
                        cols = slice(j * GW, (j + 1) * GW)
                        done(f"{name}{j}", dve.tensor_tensor(proj_w[:, w, 1, cols], bank[2 + 2 * w + j][:, :],
                                                             proj_w[:, w, 0, cols].bitcast(fp32), ALU.subtract))
                dve.wait_ge(a, act_at["rs"])
                dve.wait_ge(load_s, 64)
                done("nw1", dve.tensor_tensor(nw[:, :], rs[:, :], rs[:, :], ALU.mult))
                after("nw1")
                done("nw2", dve.tensor_tensor(nw[:, :], nw[:, :], var[:, :], ALU.mult))
                after("nw2")
                done("nw3", dve.tensor_scalar(nw[:, :], nw[:, :], -0.5, 1.5, ALU.mult, ALU.add))
                after("nw3")
                done("rstd", dve.tensor_tensor(rstd[:, :], rs[:, :], nw[:, :], ALU.mult))
                after("rstd")
                for t in range(NT):
                    done(f"xn{t}", dve.tensor_scalar(xn[:, t, :], x_in[:, t, :], mv[:, t, 0:1], rstd[:, t:t + 1],
                                                     ALU.subtract, ALU.mult))
                for m in range(4):
                    dve.wait_ge(a, act_at[f"xT{m}"])
                    src = xT[:, m * 512:(m + 1) * 512].rearrange("p (b t) -> p b t", b=2)
                    hi, lo = xT_all[:, 2 * m:2 * m + 2, 0, :], xT_all[:, 2 * m:2 * m + 2, 1, :]
                    done(f"xTh{m}", dve.tensor_copy(hi, src))
                    after(f"xTh{m}")
                    done(f"xTl{m}", dve.tensor_tensor(lo, src, hi.bitcast(fp32), ALU.subtract))
                dve.wait_ge(pe_s, pe_at["logits"])
                lg = bank[2][:, 0:NT * (H + E)].rearrange("p (t c) -> p t c", t=NT)
                done("gmax", dve.tensor_reduce(gmax[:, :], lg[:, :, H:H + E], AX.X, ALU.max))
                after("gmax")
                done("gsh", dve.tensor_tensor(gsh[:, :, :], lg[:, :, H:H + E], bc(gmax[:, :].unsqueeze(2), P, NT, E),
                                              ALU.subtract))
                done("z", dve.tensor_tensor(z[:, :, :], lg[:, :, 0:H], bc(bg_in[:, :].unsqueeze(1), P, NT, H), ALU.add))
                after("z")
                done("zn", dve.tensor_scalar(zn[:, :, :], z[:, :, :], -1.0, 0.0, ALU.mult, ALU.max))
                after("zn")
                done("za", dve.scalar_tensor_tensor(out=za[:, :, :], in0=zn[:, :, :], scalar=2.0, in1=z[:, :, :],
                                                    op0=ALU.mult, op1=ALU.add))
                dve.wait_ge(a, act_at["gexp"])
                done("gsum", dve.reduce_sum(gsum[:, :], gsh[:, :, :], AX.X))
                after("gsum")
                done("ginv", dve.reciprocal(ginv[:, :], gsum[:, :]))
                after("ginv")
                done("probs", dve.tensor_tensor(
                    probs[:, :, :, :].rearrange("p h b e -> p b h e"),
                    gsh[:, :, :].rearrange("p (b h) e -> p b h e", h=HT),
                    bc(ginv[:, :].rearrange("p (b h) -> p b h", h=HT).unsqueeze(3), P, B, HT, E), ALU.mult))
                dve.wait_ge(a, act_at["zln"])
                done("logg", dve.tensor_tensor(logg[:, :, :], za[:, :, :], zn[:, :, :], ALU.add))
                dve.wait_ge(a, act_at["xh"])
                done("xl", dve.tensor_tensor(xn_l[:, :, :], xn[:, :, :], xn_h[:, :, :], ALU.subtract))
                done("cross_c", dve.tensor_scalar(cross_c[:, :], gain_in[:, :], 1.0 / (UNIT * UNIT), None, ALU.mult))
                done("score_c", dve.tensor_scalar(score_c[:, :], gain_in[:, :], 1.0 / (math.sqrt(P) * UNIT * UNIT), None, ALU.mult))
                dve.wait_ge(pe_s, pe_at["probsT"])
                done("pT", dve.tensor_copy(pT[0][:, :], bank[6][0:B * E, 0:T]))
                after("pT")
                for r in range(K // TOPS):
                    src, dst = pT[r % 2], pT[(r + 1) % 2]
                    found = top[:, 0, r * TOPS:(r + 1) * TOPS]
                    done(f"top{r}", dve.max(found, src[:, :]))
                    after(f"top{r}")
                    done(f"idx{r}", dve.max_index(top_i[:, r * TOPS:(r + 1) * TOPS], found, src[:, :]))
                    if r < K // TOPS - 1:
                        done(f"cut{r}", dve.match_replace(dst[:, :], found, src[:, :], -1.0))
                        after(f"cut{r}")
                for j in range(2):
                    dve.wait_ge(a, act_at[f"n{j}"])
                    cols = slice(j * GW, (j + 1) * GW)
                    done(f"n{j}", dve.tensor_tensor(proj_w[:, 2, 1, cols], bank[3 + j][:, :],
                                                    proj_w[:, 2, 0, cols].bitcast(fp32), ALU.subtract))
                dve.wait_ge(a, act_at["decay3"])
                flat = decay[:, :, :, :].rearrange("p b h k -> p (b h k)")
                done("decay", dve.tensor_scalar(flat, flat, cross_c[:, 0:1], None, ALU.mult))
                done("top_copy", dve.tensor_copy(top[:, 1, :], top[:, 0, :]))
                after(f"idx{K // TOPS - 1}")
                done("tokf", dve.tensor_copy(top_t[:, 0, :], top_i[:, :]))
                done("tokf2", dve.tensor_copy(top_t[:, 1, :], top_i[:, :]))
                dve.wait_ge(made, 12)
                rows = ident[0:B * E, 0:B * E].rearrange("p (b e) -> p b e", b=B)
                done("emask", dve.reduce_sum(emask[:, :], rows.rearrange("p b e -> p e b"), AX.X))
                done("bmask", dve.reduce_sum(bmask[:, :], rows, AX.X))
                after("bmask")
                done("spread", dve.tensor_tensor(
                    tok_spread[:, :].rearrange("p (e k) -> p e k", e=E), bc(top_t[:, 0, :].unsqueeze(1), B * E, E, K),
                    bc(emask[:, :].unsqueeze(2), B * E, E, K), ALU.mult))
                done("pick", dve.tensor_copy(pick_b[:, :, :], bc(bmask[:, :].unsqueeze(2), B * E, B, P)))
                dve.wait_ge(pe_s, pe_at["slots"])
                for what, dst, at in (("gate", slot_gate, 0), ("tok", slot_tok, 64)):
                    for odd in range(2):
                        rows = slice(odd * K, (odd + 1) * K)
                        src = bank[7][rows, at:at + B * E].rearrange("p (bp o e) -> p o e bp", o=2, e=E)[:, odd]
                        done(f"{what}{odd}", dve.tensor_scalar(dst[rows, :, :], src, float(T * odd * (at > 0)), None,
                                                               ALU.add))
                done("tok_row", dve.tensor_copy(tok_row[:, :], row_i[:, :]))
                done("tok_col", dve.tensor_copy(tok_col[:, :], col_i[:, :]))
                assert n == len(steps)

        NB = 4
        with ExitStack() as c2:
            def sb2(name, shape, dt=fp32):
                return c2.enter_context(nc.sbuf_tensor(name, shape, dt))

            def sem2(name):
                return c2.enter_context(nc.semaphore(name))

            def sems2(name, n):
                return [sem2(f"{name}{i}") for i in range(n)]

            xs = sb2("xs", [P, 2, T], fp32r)
            qk = [sb2(f"qk{i}", [P, NB, GW]) for i in range(2)]
            junk = sb2("junk", [P, NB, G, P])
            ssq = [sb2(f"ssq{i}", [P, NB * G]) for i in range(2)]
            ms = sb2("ms", [P, NB * G])
            eps_c = sb2("eps_c", [P, NB * G])
            three_c = sb2("three_c", [P, NB * G])
            lms = sb2("lms", [P, NB * G])
            r0 = sb2("r0", [P, NB * G])
            nt = sb2("nt", [P, NB * G])
            vS = [sb2(f"vS{i}", [P, HT, GW]) for i in range(2)]
            qT = sb2("qT", [P, 2, G, T], fp16)
            kT = sb2("kT", [P, 2, G, T], fp16)
            sc = sb2("sc", [P, G * HT, C])
            ex = sb2("ex", [P, G * HT, C])
            smax = sb2("smax", [P, G * HT])
            ssum = sb2("ssum", [P, G * HT])
            sinv = sb2("sinv", [P, G * HT])
            AT = sb2("AT", [P, G, 3, P])

            s_zero = sem2("s_zero")
            xs_loaded = sem2("xs_loaded")
            pj = sems2("projected", 6)
            sq = sems2("squared", NB)
            raw = sems2("raw_copied", NB)
            vcp = sems2("v_copied", 2)
            mean = sems2("mean_sq", 2)
            lnm = sems2("ln_mean", 2)
            rsq = sems2("rsqrt", 2)
            newt = sem2("newton")
            nrm = sems2("normalised", 2)
            tr = sems2("transposed", NB)
            hi_s = sems2("hi_copied", NB)
            lo_s = sems2("lo_copied", NB)
            cross_s = sems2("cross_scores", 2)
            diag_s = sem2("chunk_scores")
            masked = sem2("masked")
            maxed = sem2("maxed")
            shifted = sem2("shifted")
            exped = sem2("exped")
            summed = sem2("summed")
            inverted = sem2("inverted")
            attn_s = sem2("attn_ready")
            ta = sem2("attn_turned")
            at_s = sem2("attn_T_copied")
            crossed = sems2("cross_weights", 2)
            av = sem2("weighted_values")
            summed_out = sem2("residual_added")

            PJB = [bank[0], bank[1], bank[6]]
            TRB = [bank[2], bank[3]]
            DB, XB, OB = bank[4], bank[5], bank[7]

            block = c2.enter_context(nc.Block())

            @block.sync
            def _(sp):
                src = xT_all[:, :, :, :].bitcast(fp32).rearrange("p b c t -> p b (c t)")
                dst = xs[:, :, :].bitcast(fp32).rearrange("p c t -> p (c t)")
                sp.dma_start(dst, src[:, 0, :]).then_inc(xs_loaded, 16)
                with sp.Fori(1, B) as b:
                    sp.wait_ge(pj[5], 2 * b)
                    sp.dma_start(dst, src[:, ds(b, 1), :].rearrange("p o t -> p (o t)")).then_inc(xs_loaded, 16)
                sp.wait_ge(xs_loaded, 16 * B)

            @block.tensor
            def _(pe):
                def project(b, g, k, fresh=False):
                    u = 2 * b + g
                    pe.wait_ge(xs_loaded, 16 * b + 16)
                    tile, w = (k // 2, k % 2) if k < NB else (k - NB, 2)
                    if k >= 3:
                        pe.wait_ge(raw[k - 3], u + 1)
                    elif not fresh:
                        pe.wait_ge((raw[3], vcp[0], vcp[1])[k], u)
                    for n, (a_, b_) in enumerate(((1, 0), (0, 1), (0, 0))):
                        mm = pe.matmul(PJB[k % 3][:, :], xs[:, a_, tile * P:(tile + 1) * P],
                                       proj_w[:, w, b_, g * GW:(g + 1) * GW], start=(n == 0), stop=(n == 2))
                    mm.then_inc(pj[k], 1)

                def turn(b, g, k, fresh=False):
                    u = 2 * b + g
                    pe.wait_ge(nrm[k // 2], u + 1)
                    if k >= 2:
                        pe.wait_ge(lo_s[k - 2], u + 1)
                    elif not fresh:
                        pe.wait_ge(lo_s[k + 2], u)
                    for h in range(G):
                        mm = pe.transpose(TRB[k % 2][:, h * P:(h + 1) * P], qk[g][:, k, h * P:(h + 1) * P], ident[:, :])
                    mm.then_inc(tr[k], 1)

                PARTS = ((1, 0), (0, 1), (0, 0))

                def cross(b, g, n, fresh=False):
                    u = 2 * b + g
                    if n == 0:
                        pe.wait_ge(lo_s[NB - 1], u + 1)
                        if not fresh:
                            pe.wait_ge(crossed[1], u)
                    else:
                        pe.wait_ge(crossed[0], u + 1)
                    for hh in range(2):
                        h, o = 2 * n + hh, hh * T
                        for m, (a_, b_) in enumerate(PARTS):
                            pe.matmul(XB[:, o:o + 3 * C], kT[:, a_, h, 0:P], qT[:, b_, h, C:T],
                                      start=(m == 0), stop=(m == 2))
                        for m, (a_, b_) in enumerate(PARTS):
                            mm = pe.matmul(XB[0:C, o + 3 * C:o + T], kT[:, a_, h, P:P + C], qT[:, b_, h, 3 * C:T],
                                           start=(m == 0), stop=(m == 2))
                    mm.then_inc(cross_s[n], 1)

                def chunk(b, g, fresh=False):
                    if not fresh:
                        pe.wait_ge(at_s, 2 * b + g)
                    for h in range(G):
                        for t in range(HT):
                            for c in range(2):
                                o = t * P + c * C
                                for m, (a_, b_) in enumerate(PARTS):
                                    mm = pe.matmul(DB[c * C:(c + 1) * C, (h * HT + t) * C:(h * HT + t + 1) * C],
                                                   qT[:, a_, h, o:o + C], kT[:, b_, h, o:o + C],
                                                   start=(m == 0), stop=(m == 2))
                    mm.then_inc(diag_s, 1)

                def turn_attn(b, g):
                    pe.wait_ge(attn_s, 2 * b + g + 1)
                    for h in range(G):
                        mm = pe.transpose(DB[:, h * P:(h + 1) * P], ex[:, h * HT:(h + 1) * HT, :].rearrange("p t s -> p (t s)"),
                                          ident[:, :])
                    mm.then_inc(ta, 1)

                def values(b, g, h, fresh=False):
                    u = 2 * b + g
                    if h == 0:
                        pe.wait_ge(at_s, u + 1)
                        pe.wait_ge(crossed[1], u + 1)
                        pe.wait_ge(vcp[1], u + 1)
                        if g == 0 and not fresh:
                            pe.wait_ge(summed_out, b)
                    for n, (blk, src, dst) in enumerate(((0, 0, 0), (2, 0, 1), (1, 1, 1))):
                        mm = pe.matmul(OB[:, dst * D:(dst + 1) * D], AT[:, h, blk, :],
                                       vS[g][:, src, h * P:(h + 1) * P], start=(g == 0 and h == 0 and n == 0),
                                       stop=(g == 1 and h == G - 1 and n > 0), skip_group_check=True)
                    if h == G - 1:
                        mm.then_inc(av, 1)

                def step(b, g, first=False, last=False, fresh1=False):
                    nb, ng = (b, 1) if g == 0 else (b + 1, 0)
                    pb, pg = (b, 0) if g == 1 else (b - 1, 1)
                    turn(b, g, 0, first)
                    if not last:
                        project(nb, ng, 0)
                    turn(b, g, 1, first)
                    if not last:
                        project(nb, ng, 1)
                    turn(b, g, 2)
                    if not last:
                        project(nb, ng, 2)
                    if not first:
                        turn_attn(pb, pg)
                    turn(b, g, 3)
                    if not first:
                        values(pb, pg, 0, fresh1)
                    if not last:
                        project(nb, ng, 3)
                    if not first:
                        values(pb, pg, 1)
                        values(pb, pg, 2)
                    if not last:
                        project(nb, ng, 4)
                    if not first:
                        values(pb, pg, 3)
                    if not last:
                        project(nb, ng, 5)
                    cross(b, g, 0, first)
                    chunk(b, g, first)
                    cross(b, g, 1)

                for k in range(6):
                    project(0, 0, k, fresh=True)
                step(0, 0, first=True)
                step(0, 1, fresh1=True)
                step(1, 0)
                with pe.Fori(1, B - 1) as j:
                    step(j, 1)
                    step(j + 1, 0)
                step(B - 1, 1, last=True)
                turn_attn(B - 1, 1)
                for h in range(G):
                    values(B - 1, 1, h)

            @block.scalar
            def _(act):
                def square(b, g, k, fresh=False):
                    u = 2 * b + g
                    act.wait_ge(pj[k], u + 1)
                    if not fresh:
                        act.wait_ge(sq[k], u)
                        act.wait_ge(nrm[k // 2], u - 1)
                    for h in range(G):
                        ins = act.activation(junk[:, k, h, :], PJB[k % 3][:, h * P:(h + 1) * P], ACT.Square,
                                             accum_out=ssq[g][:, k * G + h:k * G + h + 1])
                    ins.then_inc(sq[k], 1)

                def rsqrt(b, g, t):
                    u = 2 * b + g
                    cols = slice(t * 2 * G, (t + 1) * 2 * G)
                    act.wait_ge(mean[t], u + 1)
                    act.activation(lms[:, cols], ms[:, cols], ACT.Ln, scale=1.0 / P).then_inc(lnm[t], 1)
                    act.wait_ge(lnm[t], u + 1)
                    act.activation(r0[:, cols], lms[:, cols], ACT.Exp, scale=-0.5).then_inc(rsq[t], 1)

                def hi(b, g, k):
                    dst = (qT, kT)[k % 2][:, 0, :, (k // 2) * P:(k // 2 + 1) * P]
                    act.wait_ge(tr[k], 2 * b + g + 1)
                    act.activation(dst, TRB[k % 2][:, :].rearrange("p (h t) -> p h t", h=G), ACT.Copy)\
                       .then_inc(hi_s[k], 1)

                def value(b, g, t, fresh=False):
                    u = 2 * b + g
                    act.wait_ge(pj[NB + t], u + 1)
                    if not fresh:
                        act.wait_ge(av, u - 1)
                    act.activation(vS[g][:, t, :], PJB[1 + t][:, :], ACT.Copy).then_inc(vcp[t], 1)

                def exps(b, g):
                    act.wait_ge(shifted, 2 * b + g + 1)
                    act.activation(ex[:, :, :], sc[:, :, :], ACT.Exp).then_inc(exped, 1)

                def attn_T(b, g):
                    act.wait_ge(ta, 2 * b + g + 1)
                    for t in range(HT):
                        for c in range(2):
                            rows = slice(c * C, (c + 1) * C)
                            ins = act.activation(AT[rows, :, t, rows],
                                                 DB[t * C:(t + 1) * C, :].rearrange("p (h c) -> p h c", h=G)[:, :, rows],
                                                 ACT.Copy)
                    ins.then_inc(at_s, 1)

                def step(b, g, first=False, last=False, fresh=False):
                    nb, ng = (b, 1) if g == 0 else (b + 1, 0)
                    pb, pg = (b, 0) if g == 1 else (b - 1, 1)
                    hi(b, g, 0)
                    if not first:
                        exps(pb, pg)
                    if not last:
                        square(nb, ng, 0, fresh)
                    hi(b, g, 1)
                    if not last:
                        square(nb, ng, 1, fresh)
                        rsqrt(nb, ng, 0)
                    hi(b, g, 2)
                    if not first:
                        attn_T(pb, pg)
                    hi(b, g, 3)
                    if not last:
                        square(nb, ng, 2, fresh)
                        square(nb, ng, 3, fresh)
                        value(nb, ng, 0, fresh)
                        rsqrt(nb, ng, 1)
                        value(nb, ng, 1, fresh)

                act.preload_act_table_set("natural_log_exp_and_others")
                act.wait_ge(s_zero, 4)
                for k in range(NB):
                    square(0, 0, k, fresh=True)
                    if k % 2:
                        rsqrt(0, 0, k // 2)
                for t in range(HT):
                    value(0, 0, t, fresh=True)
                step(0, 0, first=True, fresh=True)
                step(0, 1)
                step(1, 0)
                with act.Fori(1, B - 1) as j:
                    step(j, 1)
                    step(j + 1, 0)
                step(B - 1, 1, last=True)
                exps(B - 1, 1)
                attn_T(B - 1, 1)

            @block.gpsimd
            def _(pool):
                pool.memset(AT[:, :, :, :], 0.0).then_inc(s_zero, 1)
                pool.memset(junk[:, :, :, :], 0.0).then_inc(s_zero, 1)
                pool.memset(eps_c[:, :], P * RMS_EPS).then_inc(s_zero, 1)
                pool.memset(three_c[:, :], 3.0 * P).then_inc(s_zero, 1)
                pool.wait_ge(s_zero, 4)

                def normalise(b, g, t):
                    u = 2 * b + g
                    cols = slice(t * 2 * G, (t + 1) * 2 * G)
                    pool.wait_ge(sq[2 * t + 1], u + 1)
                    pool.tensor_tensor(ms[:, cols], ssq[g][:, cols], eps_c[:, cols], ALU.add).then_inc(mean[t], 1)
                    n0 = 8 * u + 4 * t
                    pool.wait_ge(rsq[t], u + 1)
                    pool.tensor_tensor(nt[:, cols], r0[:, cols], r0[:, cols], ALU.mult).then_inc(newt, 1)
                    pool.wait_ge(newt, n0 + 1)
                    pool.tensor_tensor(nt[:, cols], nt[:, cols], ms[:, cols], ALU.mult).then_inc(newt, 1)
                    pool.wait_ge(newt, n0 + 2)
                    pool.tensor_tensor(nt[:, cols], three_c[:, cols], nt[:, cols], ALU.subtract).then_inc(newt, 1)
                    pool.wait_ge(newt, n0 + 3)
                    pool.tensor_tensor(nt[:, cols], nt[:, cols], r0[:, cols], ALU.mult).then_inc(newt, 1)
                    pool.wait_ge(newt, n0 + 4)
                    pool.wait_ge(raw[2 * t + 1], u + 1)
                    rows = qk[g][:, 2 * t:2 * t + 2, :].rearrange("p k (h d) -> p (k h) d", h=G)
                    pool.tensor_tensor(rows, rows, bc(nt[:, cols].unsqueeze(2), P, 2 * G, P), ALU.mult)\
                        .then_inc(nrm[t], 1)

                with pool.Fori(0, B) as b:
                    for g in range(2):
                        for t in range(HT):
                            normalise(b, g, t)

            @block.vector
            def _(dve):
                def raw_copy(b, g, k):
                    dve.wait_ge(sq[k], 2 * b + g + 1)
                    dve.tensor_copy(qk[g][:, k, :], PJB[k % 3][:, :]).then_inc(raw[k], 1)

                def lo(b, g, k):
                    cols = slice((k // 2) * P, (k // 2 + 1) * P)
                    w = (qT, kT)[k % 2]
                    dve.wait_ge(hi_s[k], 2 * b + g + 1)
                    dve.tensor_tensor(w[:, 1, :, cols], TRB[k % 2][:, :].rearrange("p (h t) -> p h t", h=G),
                                      w[:, 0, :, cols], ALU.subtract).then_inc(lo_s[k], 1)

                def softmax_shift(b, g):
                    u = 2 * b + g
                    dve.wait_ge(diag_s, u + 1)
                    dve.scalar_tensor_tensor(out=sc[:, :, :], in0=DB[:, :].rearrange("p (h s) -> p h s", s=C),
                                             scalar=score_c[:, 0:1], in1=bc(causal[:, :].unsqueeze(1), P, G * HT, C),
                                             op0=ALU.mult, op1=ALU.add).then_inc(masked, 1)
                    dve.wait_ge(masked, u + 1)
                    dve.tensor_reduce(smax[:, :], sc[:, :, :], AX.X, ALU.max).then_inc(maxed, 1)
                    dve.wait_ge(maxed, u + 1)
                    dve.tensor_tensor(sc[:, :, :], sc[:, :, :], bc(smax[:, :].unsqueeze(2), P, G * HT, C),
                                      ALU.subtract).then_inc(shifted, 1)

                def softmax_norm(b, g):
                    u = 2 * b + g
                    dve.wait_ge(exped, u + 1)
                    dve.reduce_sum(ssum[:, :], ex[:, :, :], AX.X).then_inc(summed, 1)
                    dve.wait_ge(summed, u + 1)
                    dve.reciprocal(sinv[:, :], ssum[:, :]).then_inc(inverted, 1)
                    dve.wait_ge(inverted, u + 1)
                    dve.tensor_tensor(ex[:, :, :], ex[:, :, :], bc(sinv[:, :].unsqueeze(2), P, G * HT, C), ALU.mult)\
                       .then_inc(attn_s, 1)

                def cross_weights(b, g, n):
                    dve.wait_ge(cross_s[n], 2 * b + g + 1)
                    src = XB[:, :].rearrange("p (h t) -> p h t", h=2)
                    heads = slice(2 * n, 2 * n + 2)
                    ends = XB[0:C, :].rearrange("p (h k t) -> p h k t", h=2, t=C)[:, :, 0:4:3, :]
                    dve.tensor_scalar(AT[0:C, heads, 0:2, C:P], ends, cross_c[0:C, 0:1], None, ALU.mult)
                    w = decay[:, ds(b, 1), g * G + 2 * n:g * G + 2 * n + 2, :].rearrange("p o h k -> p (o h) k")
                    dve.tensor_tensor(AT[:, heads, 2, :].rearrange("p h (k t) -> p h k t", k=2),
                                      src[:, :, C:3 * C].rearrange("p h (k t) -> p h k t", k=2),
                                      bc(w.unsqueeze(3), P, 2, 2, C), ALU.mult).then_inc(crossed[n], 1)

                def residual(b):
                    dve.wait_ge(av, 2 * b + 2)
                    rows = x_in[:, ds(HT * b, HT), :].rearrange("p h d -> p (h d)")
                    dve.tensor_tensor(rows, rows, OB[:, 0:T], ALU.add).then_inc(summed_out, 1)

                def step(b, g, first=False, last=False):
                    nb, ng = (b, 1) if g == 0 else (b + 1, 0)
                    pb, pg = (b, 0) if g == 1 else (b - 1, 1)
                    if not first:
                        softmax_shift(pb, pg)
                    lo(b, g, 0)
                    if not first:
                        softmax_norm(pb, pg)
                    lo(b, g, 1)
                    if not last:
                        raw_copy(nb, ng, 0)
                    if not first:
                        cross_weights(pb, pg, 1)
                    if not last:
                        raw_copy(nb, ng, 1)
                    lo(b, g, 2)
                    lo(b, g, 3)
                    if not last:
                        raw_copy(nb, ng, 2)
                        raw_copy(nb, ng, 3)
                    if g == 0 and not first:
                        residual(pb)
                    cross_weights(b, g, 0)

                dve.wait_ge(s_zero, 4)
                for k in range(NB):
                    raw_copy(0, 0, k)
                step(0, 0, first=True)
                step(0, 1)
                step(1, 0)
                with dve.Fori(1, B - 1) as j:
                    step(j, 1)
                    step(j + 1, 0)
                step(B - 1, 1, last=True)
                softmax_shift(B - 1, 1)
                cross_weights(B - 1, 1, 1)
                softmax_norm(B - 1, 1)
                residual(B - 1)

        with ExitStack() as c3:
            def sb3(name, shape, dt=fp32):
                return c3.enter_context(nc.sbuf_tensor(name, shape, dt))

            def sem3(name):
                return c3.enter_context(nc.semaphore(name))

            def sems3(name, n):
                return [sem3(f"{name}{i}") for i in range(n)]

            NSLOT = B * K
            onehot = [sb3(f"onehot{i}", [P, HT, E * K], fp16) for i in range(2)]
            picked = sb3("picked", [P, 2, E, NSLOT], fp32r)
            w1_in = [sb3(f"w1_in{i}", [P, F]) for i in range(2)]
            w1_hl = [sb3(f"w1_hl{i}", [P, 2, F], fp32r) for i in range(2)]
            w2_in = [sb3(f"w2_in{i}", [P, FT, D]) for i in range(2)]
            hid = [sb3(f"hid{i}", [P, FT, NSLOT]) for i in range(2)]
            back = [sb3(f"back{i}", [P, BP, 2 * T], fp32r) for i in range(2)]
            y = [sb3(f"y{i}", [P, BP, D]) for i in range(2)]
            y_hl = [sb3(f"y_hl{i}", [P, 2, BP, D], fp32r) for i in range(2)]
            moe = sb3("moe", [P, NT * P], bf16)
            res = sb3("res", [P, NT, D])

            asked = sem3("tokens_spread")
            hot = sem3("onehots")
            gath = sem3("gathered")
            gath_h = sem3("gathered_hi")
            gath_l = sem3("gathered_lo")
            w1_s = sems3("w1_loaded", 2)
            w2_s = sems3("w2_loaded", 2)
            w1h_s = sems3("w1_hi", 2)
            w1l_s = sems3("w1_lo", 2)
            up = sems3("up_done", FT)
            gelu = sems3("gelu_done", FT)
            down = sem3("down_done")
            gated = sem3("gated")
            y_hi = sem3("y_hi")
            y_lo = sem3("y_lo")
            back_s = sem3("scatter_ready")
            scat = sem3("scattered")
            moe_s = sem3("moe_rounded")
            moe_t = sem3("moe_turned")
            res_s = sem3("summed_up")
            out_s = sem3("stored")

            ACC = bank[0:4]
            UPB = [bank[4], bank[5]]
            YB = [bank[6], bank[7]]
            block = c3.enter_context(nc.Block())
            out_v = out.rearrange("b (h p) d -> p (b h) d", p=P)

            @block.sync
            def _(sp):
                def load(e, par):
                    sp.dma_start(w1_in[par][:, :], w1[ds(e, 1), :, :].rearrange("o d f -> d (o f)"))\
                      .then_inc(w1_s[par], 16)
                    sp.dma_start(w2_in[par][:, :, :], w2[ds(e, 1), :, :].rearrange("o (f p) d -> p (o f) d", p=P))\
                      .then_inc(w2_s[par], 16)

                for par in range(2):
                    load(par, par)
                with sp.Fori(1, E // 2) as j:
                    for par in range(2):
                        sp.wait_ge(w1l_s[par], j)
                        sp.wait_ge(down, 2 * j + par - 1)
                        load(2 * j + par, par)
                for m in range(4):
                    sp.wait_ge(res_s, m + 1)
                    sp.dma_start(out_v[:, 4 * m:4 * m + 4, :], res[:, 4 * m:4 * m + 4, :]).then_inc(out_s, 16)
                for par in range(2):
                    sp.wait_ge(w1_s[par], 16 * (E // 2))
                    sp.wait_ge(w2_s[par], 16 * (E // 2))
                sp.wait_ge(out_s, 64)

            @block.tensor
            def _(pe):
                def gather(j, first=False):
                    for k in range(2):
                        if not first:
                            pe.wait_ge(hot, 2 * j)
                        pe.matmul(bank[k][:, :], pick_b[:, ds(2 * j + k, 1), :].rearrange("p o t -> p (o t)"),
                                  tok_spread[:, :], start=True, stop=True).then_inc(asked, 1)
                    for k in range(2):
                        b = 2 * j + k
                        pe.wait_ge(hot, b + 1)
                        if not first:
                            pe.wait_ge(gath_l, 2 * j)
                        for n, (rows, t) in enumerate(((xn_l, 0), (xn_l, 1), (xn_h, 0), (xn_h, 1))):
                            mm = pe.matmul(bank[2 + k][:, :], rows[:, ds(HT * b + t, 1), :].rearrange("p o d -> p (o d)"),
                                           onehot[k][:, t, :], start=(n == 0), stop=(n == 3))
                        mm.then_inc(gath, 1)

                gather(0, first=True)
                with pe.Fori(1, B // 2) as j:
                    gather(j)
                pe.wait_ge(gath_l, B)

                def ups(e, par, j):
                    pe.wait_ge(w1l_s[par], j + 1)
                    for f in range(FT):
                        if f >= 2:
                            pe.wait_ge(gelu[f - 2], e + 1)
                        elif not isinstance(e, int) or e:
                            pe.wait_ge(gelu[f + 2], e)
                        for n, (a_, b_) in enumerate(((1, 0), (0, 1), (0, 0))):
                            mm = pe.matmul(UPB[f % 2][:, :], w1_hl[par][:, a_, f * P:(f + 1) * P],
                                           picked[:, b_, ds(e, 1), :].rearrange("p o s -> p (o s)"),
                                           start=(n == 0), stop=(n == 2))
                        mm.then_inc(up[f], 1)

                def downs(e, par, j):
                    pe.wait_ge(gelu[FT - 1], e + 1)
                    pe.wait_ge(w2_s[par], 16 * j + 16)
                    if not isinstance(e, int) or e >= 2:
                        pe.wait_ge(gated, e - 1)
                    for s in range(BP):
                        for f in range(FT):
                            mm = pe.matmul(YB[par][:, s * D:(s + 1) * D], hid[par][:, f, s * P:(s + 1) * P],
                                           w2_in[par][:, f, :], start=(f == 0), stop=(f == FT - 1))
                    mm.then_inc(down, 1)

                def scatter(e, par, first=False):
                    pe.wait_ge(y_lo, e + 1)
                    pe.wait_ge(back_s, BP * e + BP)
                    for s in range(BP):
                        for n in (1, 0):
                            mm = pe.matmul(ACC[s][:, :], y_hl[par][:, n, s, :], back[par][:, s, :],
                                           start=(first and n == 1), stop=True, skip_group_check=True)
                    mm.then_inc(scat, 1)

                ups(0, 0, 0)
                ups(1, 1, 0)
                downs(0, 0, 0)
                ups(2, 0, 1)
                scatter(0, 0, first=True)
                downs(1, 1, 0)
                ups(3, 1, 1)
                scatter(1, 1)
                downs(2, 0, 1)
                with pe.Fori(2, E // 2) as j:
                    ups(2 * j, 0, j)
                    scatter(2 * j - 2, 0)
                    downs(2 * j - 1, 1, j - 1)
                    ups(2 * j + 1, 1, j)
                    scatter(2 * j - 1, 1)
                    downs(2 * j, 0, j)
                scatter(E - 2, 0)
                downs(E - 1, 1, E // 2 - 1)
                scatter(E - 1, 1)
                for m in range(4):
                    pe.wait_ge(moe_s, m + 1)
                    for t in range(4):
                        mm = pe.transpose(bank[4 + m][:, :].bitcast(bf16)[:, t * P:(t + 1) * P],
                                          moe[:, (4 * m + t) * P:(4 * m + t + 1) * P], ident_b[:, :])
                    mm.then_inc(moe_t, 1)

            @block.scalar
            def _(act):
                with act.Fori(0, B // 2) as j:
                    for k in range(2):
                        b = 2 * j + k
                        act.wait_ge(gath, b + 1)
                        act.activation(picked[:, 0, :, ds(K * b, K)], bank[2 + k][:, :].rearrange("p (e s) -> p e s", e=E),
                                       ACT.Copy).then_inc(gath_h, 1)
                def gelus(j, first=False):
                    for par in range(2):
                        e = 2 * j + par
                        for f in range(FT):
                            act.wait_ge(up[f], e + 1)
                            if f == 0 and not first:
                                act.wait_ge(down, e - 1)
                            act.activation(hid[par][:, f, :], UPB[f % 2][:, :], ACT.Gelu_apprx_tanh)\
                               .then_inc(gelu[f], 1)

                gelus(0, first=True)
                with act.Fori(1, E // 2) as j:
                    gelus(j)
                act.wait_ge(scat, E)
                for m in range(4):
                    act.activation(moe[:, m * 512:(m + 1) * 512], ACC[m][:, :], ACT.Copy).then_inc(moe_s, 1)

            @block.vector
            def _(dve):
                def split_w1(par, j, first=False):
                    dve.wait_ge(w1_s[par], 16 * j + 16)
                    if not first:
                        dve.wait_ge(up[FT - 1], 2 * j + par - 1)
                    dve.tensor_copy(w1_hl[par][:, 0, :], w1_in[par][:, :]).then_inc(w1h_s[par], 1)
                    dve.wait_ge(w1h_s[par], j + 1)
                    dve.tensor_tensor(w1_hl[par][:, 1, :], w1_in[par][:, :], w1_hl[par][:, 0, :].bitcast(fp32),
                                      ALU.subtract).then_inc(w1l_s[par], 1)

                def gather(j, first=False):
                    for k in range(2):
                        dve.wait_ge(asked, 2 * j + k + 1)
                        if not first:
                            dve.wait_ge(gath, 2 * j)
                        for t in range(HT):
                            ins = dve.tensor_scalar(onehot[k][:, t, :], bank[k][:, :], tok_col[:, t:t + 1], None,
                                                    ALU.is_equal)
                        ins.then_inc(hot, 1)
                    for k in range(2):
                        b = 2 * j + k
                        dve.wait_ge(gath_h, b + 1)
                        dve.tensor_tensor(picked[:, 1, :, ds(K * b, K)],
                                          bank[2 + k][:, :].rearrange("p (e s) -> p e s", e=E),
                                          picked[:, 0, :, ds(K * b, K)].bitcast(fp32), ALU.subtract).then_inc(gath_l, 1)

                gather(0, first=True)
                with dve.Fori(1, B // 2) as j:
                    gather(j)
                split_w1(0, 0, first=True)
                split_w1(1, 0, first=True)

                def expert(e, par, j, peel=False):
                    for s in range(BP):
                        if s == 0 and not peel:
                            dve.wait_ge(scat, e - 1)
                        dve.tensor_scalar(back[par][:, s, :], tok_row[:, :],
                                          slot_tok[:, ds(e, 1), s:s + 1].rearrange("p o k -> p (o k)"), None,
                                          ALU.is_equal).then_inc(back_s, 1)
                    dve.wait_ge(down, e + 1)
                    dve.tensor_tensor(y[par][:, :, :], YB[par][:, :].rearrange("p (s d) -> p s d", s=BP),
                                      bc(slot_gate[:, ds(e, 1), :].rearrange("p o s -> p (o s)").unsqueeze(2), P, BP, D),
                                      ALU.mult).then_inc(gated, 1)
                    dve.wait_ge(gated, e + 1)
                    dve.tensor_copy(y_hl[par][:, 0, :, :], y[par][:, :, :]).then_inc(y_hi, 1)
                    dve.wait_ge(y_hi, e + 1)
                    dve.tensor_tensor(y_hl[par][:, 1, :, :], y[par][:, :, :], y_hl[par][:, 0, :, :].bitcast(fp32),
                                      ALU.subtract).then_inc(y_lo, 1)

                expert(0, 0, 0, peel=True)
                split_w1(0, 1)
                expert(1, 1, 0, peel=True)
                split_w1(1, 1)
                with dve.Fori(1, E // 2 - 1) as j:
                    for par in range(2):
                        expert(2 * j + par, par, j)
                        split_w1(par, j + 1)
                for par in range(2):
                    expert(E - 2 + par, par, E // 2 - 1)
                for m in range(4):
                    dve.wait_ge(moe_t, m + 1)
                    dve.tensor_tensor(res[:, 4 * m:4 * m + 4, :], x_in[:, 4 * m:4 * m + 4, :],
                                      bank[4 + m][:, :].bitcast(bf16)[:, 0:512].rearrange("p (t d) -> p t d", t=4),
                                      ALU.add).then_inc(res_s, 1)


_INS = ['L0_attn_x', 'L0_attn_Wq', 'L0_attn_Wk', 'L0_attn_Wv', 'L0_attn_Wg', 'L0_attn_bg', 'L0_attn_Wo',
        'L0_attn_qk_gain', 'L0_ffn_gate_w', 'L0_ffn_w1', 'L0_ffn_w2']
_OUTS = [((8, 256, 128), 'float32')]


def kernel(**inputs):
    import numpy as _np
    import concourse.bacc as _bacc
    from concourse import mybir as _mybir
    from concourse.bass_utils import run_bass_kernel_spmd as _run

    nc = _bacc.Bacc("TRN2", target_bir_lowering=False, num_devices=1)
    arrays, args = {}, []
    for name in _INS:
        a = _np.ascontiguousarray(inputs[name])
        if name == 'L0_attn_qk_gain':
            a = a.reshape(1)
        arrays[f"in_{name}_dram"] = a
        args.append(nc.dram_tensor(f"in_{name}_dram", a.shape, _mybir.dt.from_np(a.dtype), kind="ExternalInput").ap())
    for i, (shape, dtype) in enumerate(_OUTS):
        dt = _mybir.dt.from_np(_np.dtype(dtype))
        args.append(nc.dram_tensor(f"out_{i}_dram", shape, dt, kind="ExternalOutput").ap())
    norm_attention_and_expert_choice_ffn_kernel(nc, *args)
    r = _run(nc, [arrays], core_ids=[0])
    got = tuple(r.results[0][f"out_{i}_dram"] for i in range(len(_OUTS)))
    return got[0]
```

```python
import math
import concourse.bass as bass
from concourse import mybir
from contextlib import ExitStack


def norm_attention_and_expert_choice_ffn_kernel(
    nc: bass.Bass,
    x: bass.AP,
    Wq: bass.AP,
    Wk: bass.AP,
    Wv: bass.AP,
    Wg: bass.AP,
    bg: bass.AP,
    Wo: bass.AP,
    qk_gain: bass.AP,
    gate_w: bass.AP,
    w1: bass.AP,
    w2: bass.AP,
    out: bass.AP,
):
    fp32 = mybir.dt.float32
    fp32r = mybir.dt.float32r
    fp16 = mybir.dt.float16
    bf16 = mybir.dt.bfloat16
    i32 = mybir.dt.int32
    u32 = mybir.dt.uint32
    ALU = mybir.AluOpType
    ACT = mybir.ActivationFunctionType
    AX = mybir.AxisListType
    ds = bass.ds

    P = 128
    B, T, D = x.shape
    HT = T // P
    NT = B * HT
    H = Wg.shape[0]
    C = 64
    G = 4
    GW = G * P
    E = gate_w.shape[1]
    F = w1.shape[2]
    FT = F // P
    K = 2 * T // E
    BP = B * K // P
    TOPS = 8
    LN_EPS, RMS_EPS = 1e-5, 1e-6
    NEG = -1.0e30
    UNIT = 2.0 * P
    assert D == P and HT == 2 and T == 4 * C and H == 2 * G and 2 * K == P and B * E == 64 and E == H

    def bc(ap, *shape):
        return ap.broadcast_to(list(shape))

    ctx = ExitStack()
    with ctx:
        def sb(name, shape, dt=fp32):
            return ctx.enter_context(nc.sbuf_tensor(name, shape, dt))

        def sem(name):
            return ctx.enter_context(nc.semaphore(name))

        def sems(name, n):
            return [sem(f"{name}{i}") for i in range(n)]

        bank = [ctx.enter_context(nc.psum_tensor(f"bank{i}", [P, 512], fp32)) for i in range(8)]

        x_in = sb("x_in", [P, NT, D])
        xn_h = sb("xn_h", [P, NT, D], fp16)
        xn_l = sb("xn_l", [P, NT, D], fp16)
        decay = sb("decay", [P, B, H, 2])
        score_c = sb("score_c", [P, 1])
        cross_c = sb("cross_c", [P, 1])
        causal = sb("causal", [P, C])
        ident = sb("ident", [P, P])
        ident_b = sb("ident_b", [P, P], bf16)
        slot_gate = sb("slot_gate", [P, E, BP])
        slot_tok = sb("slot_tok", [P, E, BP])
        tok_spread = sb("tok_spread", [B * E, E * K], fp16)
        pick_b = sb("pick_b", [B * E, B, P], fp16)
        tok_col = sb("tok_col", [P, HT])
        tok_row = sb("tok_row", [P, HT * T])
        w1_in = sb("w1_in", [P, E, F])
        w2_in = sb("w2_in", [P, E * FT, D])
        front = ctx.enter_context(ExitStack())
        xT_all = front.enter_context(nc.sbuf_tensor("xT_all", [P, B, 2, T], fp32r))
        proj_w = front.enter_context(nc.sbuf_tensor("proj_w", [P, 3, 2, H * P], fp32r))
        left = front.enter_context(nc.sbuf_tensor("left", [B * E, T], fp32))
        emask = front.enter_context(nc.sbuf_tensor("emask", [B * E, E], fp32))

        with ExitStack() as c1:
            def sb1(name, shape, dt=fp32):
                return c1.enter_context(nc.sbuf_tensor(name, shape, dt))

            def sem1(name):
                return c1.enter_context(nc.semaphore(name))

            wq_in = sb1("wq_in", [P, H, D])
            wk_in = sb1("wk_in", [P, H, D])
            wv_in = sb1("wv_in", [P, H, D])
            wo_in = sb1("wo_in", [P, H * P])
            wo_T = sb1("wo_T", [P, H, D])
            gates_w = sb1("gates_w", [P, H + E])
            bg_in = sb1("bg_in", [P, H])
            gain_in = sb1("gain_in", [P, 1])
            stats = sb1("stats", [P, NT, 6])
            mv = sb1("mv", [P, NT, 2])
            var = sb1("var", [P, NT])
            lnv = sb1("lnv", [P, NT])
            rs = sb1("rs", [P, NT])
            nw = sb1("nw", [P, NT])
            rstd = sb1("rstd", [P, NT])
            shift = sb1("shift", [P, NT])
            xn = sb1("xn", [P, NT, D])
            xT = sb1("xT", [P, NT * P])
            z = sb1("z", [P, NT, H])
            za = sb1("za", [P, NT, H])
            zn = sb1("zn", [P, NT, H])
            logg = sb1("logg", [P, NT, H])
            later = sb1("later", [P, P])
            whole = sb1("whole", [P, P])
            gmax = sb1("gmax", [P, NT])
            gsh = sb1("gsh", [P, NT, E])
            gsum = sb1("gsum", [P, NT])
            ginv = sb1("ginv", [P, NT])
            probs = sb1("probs", [P, HT, B, E])
            bmask = sb1("bmask", [B * E, B])
            row_i = sb1("row_i", [P, HT * T], i32)
            col_i = sb1("col_i", [P, HT], i32)

            load_x = [sem1(f"load_x{m}") for m in range(4)]
            load_q, load_k, load_o, load_v = [sem1(f"load_w{c}") for c in "qkov"]
            load_s = sem1("load_s")
            made = sem1("made")
            d = sem1("dve1")
            a = sem1("act1")
            pe_s = sem1("pe1")

            dve_at, act_at, pe_at = {}, {}, {}

            DVE_TILES = 11

            block = c1.enter_context(nc.Block())

            for n, name in enumerate(["q0", "q1", "k0", "k1", "xT0", "xT1", "xT2", "xT3", "woT0", "woT1", "logits",
                                      "n0", "n1", "decay", "probsT"]):
                pe_at[name] = n + 1
            for n, name in enumerate(["ln_v", "rs", "q0", "q1"] + [f"xn{t}" for t in range(DVE_TILES, NT)] +
                                     ["k0", "k1", "xT0", "xT1", "xT2", "xT3", "woT0", "woT1", "zexp", "zln", "gexp",
                                      "n0", "n1", "decay2", "decay3"]):
                act_at[name] = n + 1
            steps = ["zero", "emask", "bmask", "pick", "tok_row", "tok_col"]
            steps += [f"st{t}" for t in range(NT)] + [f"mv{t}" for t in range(NT)]
            steps += ["var", "cross_c", "score_c", "nw1", "nw2", "nw3", "rstd", "shift"]
            steps += [f"xn{t}" for t in range(DVE_TILES)]
            steps += ["q0", "q1", "k0", "k1", "xTh0", "xTl0", "xTh1", "xTl1", "xTh2", "xTl2", "xTh3", "xTl3"]
            steps += ["z", "zn", "za", "gmax", "gsh", "logg", "gsum", "ginv", "probs", "n0", "n1", "decay", "left"]
            for n, name in enumerate(steps):
                dve_at[name] = n + 1

            @block.sync
            def _(sp):
                x_v = x.rearrange("b (h p) d -> p (b h) d", p=P)
                for m in range(4):
                    sp.dma_start(x_in[:, 4 * m:4 * m + 4, :], x_v[:, 4 * m:4 * m + 4, :]).then_inc(load_x[m], 16)
                sp.dma_start(wq_in[:, :, :], Wq.rearrange("(h p) d -> p h d", p=P)).then_inc(load_q, 16)
                sp.dma_start(wk_in[:, :, :], Wk.rearrange("(h p) d -> p h d", p=P)).then_inc(load_k, 16)
                sp.dma_start(wo_in[:, :], Wo).then_inc(load_o, 16)
                sp.dma_start(wv_in[:, :, :], Wv.rearrange("(h p) d -> p h d", p=P)).then_inc(load_v, 16)
                for loaded in (*load_x, load_q, load_k, load_o, load_v):
                    sp.wait_ge(loaded, 16)
                sp.wait_ge(load_s, 64)

            @block.gpsimd
            def _(pool):
                n = 0

                def done(ins):
                    nonlocal n
                    n += 1
                    ins.then_inc(made, 1)
                    pool.wait_ge(made, n)

                done(pool.memset(ident[:, :], 0.0))
                done(pool.affine_select(out=ident[:, :], in_=ident[:, :], compare_op=ALU.not_equal, fill=1.0, base=0,
                                        pattern=[[-1, P]], channel_multiplier=1))
                done(pool.iota(row_i[:, :], pattern=[[1, HT * T]], base=0, channel_multiplier=0))
                done(pool.iota(col_i[:, :], pattern=[[P, HT]], base=0, channel_multiplier=1))
                done(pool.memset(later[:, :], 0.0))
                done(pool.memset(whole[:, :], 0.0))
                done(pool.memset(later[C:P, 0:C], 1.0))
                done(pool.memset(whole[0:C, :], 1.0))
                done(pool.memset(causal[:, :], 0.0))
                for c in range(2):
                    rows = causal[c * C:(c + 1) * C, :]
                    done(pool.affine_select(out=rows, in_=rows, compare_op=ALU.is_ge, fill=NEG, base=0,
                                            pattern=[[-1, C]], channel_multiplier=1))
                done(pool.tensor_copy(ident_b[:, :], ident[:, :]))
                pool.wait_ge(d, dve_at[f"xn{DVE_TILES - 1}"])
                pool.wait_ge(a, act_at[f"xn{NT - 1}"])
                done(pool.tensor_copy(xn_h[:, :, :], xn[:, :, :]))
                done(pool.tensor_tensor(xn_l[:, :, :], xn[:, :, :], xn_h[:, :, :], ALU.subtract))
                assert n == 14

            @block.scalar
            def _(act):
                act.preload_act_table_set("natural_log_exp_and_others")
                act.dma_start(gates_w[:, H:H + E], gate_w).then_inc(load_s, 16)
                act.dma_start(gates_w[:, 0:H], Wg.rearrange("h d -> d h"), allow_slow_non_contiguous=True)\
                   .then_inc(load_s, 16)
                act.dma_start(bg_in[:, :], bg.partition_broadcast(P)).then_inc(load_s, 16)
                act.dma_start(gain_in[:, :], qk_gain.partition_broadcast(P)).then_inc(load_s, 16)
                n = 0

                def done(name, ins):
                    nonlocal n
                    n += 1
                    assert act_at[name] == n, name
                    ins.then_inc(a, 1)

                act.wait_ge(d, dve_at["var"])
                done("ln_v", act.activation(lnv[:, :], var[:, :], ACT.Ln))
                act.wait_ge(a, act_at["ln_v"])
                done("rs", act.activation(rs[:, :], lnv[:, :], ACT.Exp, scale=-0.5))

                def weight_hi(w, j):
                    name = f"{'qk'[w]}{j}"
                    act.wait_ge(pe_s, pe_at[name])
                    done(name, act.activation(proj_w[:, w, 0, j * GW:(j + 1) * GW], bank[2 + 2 * w + j][:, :], ACT.Copy))

                weight_hi(0, 0)
                weight_hi(0, 1)
                act.wait_ge(d, dve_at["shift"])
                for t in range(DVE_TILES, NT):
                    done(f"xn{t}", act.activation(xn[:, t, :], x_in[:, t, :], ACT.Identity, scale=rstd[:, t:t + 1],
                                                  bias=shift[:, t:t + 1]))
                weight_hi(1, 0)
                weight_hi(1, 1)
                for m in range(4):
                    act.wait_ge(pe_s, pe_at[f"xT{m}"])
                    done(f"xT{m}", act.activation(xT[:, m * 512:(m + 1) * 512], bank[(6 + m) % 8][:, :], ACT.Copy))
                for j in range(2):
                    act.wait_ge(pe_s, pe_at[f"woT{j}"])
                    done(f"woT{j}", act.activation(wo_T[:, G * j:G * (j + 1), :].rearrange("p h d -> p (h d)"),
                                                   bank[6 + j][:, :], ACT.Copy))
                act.wait_ge(d, dve_at["za"])
                done("zexp", act.activation(za[:, :, :], za[:, :, :], ACT.Exp, scale=-1.0))
                act.wait_ge(a, act_at["zexp"])
                done("zln", act.activation(za[:, :, :], za[:, :, :], ACT.Ln, bias=1.0))
                act.wait_ge(d, dve_at["gsh"])
                done("gexp", act.activation(gsh[:, :, :], gsh[:, :, :], ACT.Exp))
                for j in range(2):
                    act.wait_ge(pe_s, pe_at[f"n{j}"])
                    done(f"n{j}", act.activation(proj_w[:, 2, 0, j * GW:(j + 1) * GW], bank[3 + j][:, :], ACT.Copy))
                act.wait_ge(pe_s, pe_at["decay"])
                for k in range(2):
                    done(f"decay{2 + k}", act.activation(
                        decay[:, :, :, k].rearrange("p b h -> p (b h)"), bank[5][:, k * B * H:(k + 1) * B * H],
                        ACT.Exp, scale=-1.0))

            @block.tensor
            def _(pe):
                n = 0

                def done(name, ins):
                    nonlocal n
                    n += 1
                    assert pe_at[name] == n, name
                    ins.then_inc(pe_s, 1)

                pe.wait_ge(made, 2)
                for w, (name, w_in, loaded) in enumerate((("q", wq_in, load_q), ("k", wk_in, load_k))):
                    pe.wait_ge(loaded, 16)
                    for j in range(2):
                        for h in range(G):
                            mm = pe.transpose(bank[2 + 2 * w + j][:, h * P:(h + 1) * P], w_in[:, G * j + h, :],
                                              ident[:, :])
                        done(f"{name}{j}", mm)
                for m in range(4):
                    pe.wait_ge(d, dve_at[f"xn{min(4 * m + 3, DVE_TILES - 1)}"])
                    if 4 * m + 3 >= DVE_TILES:
                        pe.wait_ge(a, act_at[f"xn{4 * m + 3}"])
                    for t in range(4):
                        mm = pe.transpose(bank[(6 + m) % 8][:, t * P:(t + 1) * P], xn[:, 4 * m + t, :], ident[:, :])
                    done(f"xT{m}", mm)
                pe.wait_ge(load_o, 16)
                for j in range(2):
                    pe.wait_ge(a, act_at[f"xT{j}"])
                    for h in range(G):
                        mm = pe.transpose(bank[6 + j][:, h * P:(h + 1) * P], wo_in[:, (G * j + h) * P:(G * j + h + 1) * P],
                                          ident[:, :])
                    done(f"woT{j}", mm)
                pe.wait_ge(load_s, 64)
                pe.wait_ge(d, dve_at["q0"])
                for t in range(NT):
                    pe.wait_ge(a, act_at[f"xT{t // 4}"])
                    mm = pe.matmul(bank[2][:, t * (H + E):(t + 1) * (H + E)], xT[:, t * P:(t + 1) * P], gates_w[:, :],
                                   start=True, stop=True)
                done("logits", mm)
                pe.wait_ge(load_v, 16)
                for j in range(2):
                    pe.wait_ge(a, act_at[f"woT{j}"])
                    pe.wait_ge(d, dve_at[("q1", "k0")[j]])
                    for h in range(G):
                        mm = pe.matmul(bank[3 + j][:, h * P:(h + 1) * P], wv_in[:, G * j + h, :], wo_T[:, G * j + h, :],
                                       start=True, stop=True)
                    done(f"n{j}", mm)
                pe.wait_ge(made, 8)
                pe.wait_ge(d, dve_at["logg"])
                pe.wait_ge(d, dve_at["k1"])
                by_tile = logg[:, :, :].rearrange("p (b t) h -> p t b h", t=HT)
                BH = B * H
                pe.matmul(bank[5][:, 0:BH], later[:, :], by_tile[:, 0], start=True, stop=True)
                pe.matmul(bank[5][:, BH:2 * BH], later[:, :], by_tile[:, 0], start=True, stop=False)
                done("decay", pe.matmul(bank[5][:, BH:2 * BH], whole[:, :], by_tile[:, 1], start=False, stop=True))
                pe.wait_ge(d, dve_at["probs"])
                for t in range(HT):
                    mm = pe.transpose(bank[6][0:B * E, t * P:(t + 1) * P],
                                      probs[:, t, :, :].rearrange("p b e -> p (b e)"), ident[:, :])
                done("probsT", mm)
            @block.vector
            def _(dve):
                n = 0

                def done(name, ins):
                    nonlocal n
                    n += 1
                    assert dve_at[name] == n, (name, n)
                    ins.then_inc(d, 1)

                def after(name):
                    dve.wait_ge(d, dve_at[name])

                done("zero", dve.memset(mv[:, :, :], 0.0))
                dve.wait_ge(made, 2)
                rows = ident[0:B * E, 0:B * E].rearrange("p (b e) -> p b e", b=B)
                done("emask", dve.reduce_sum(emask[:, :], rows.rearrange("p b e -> p e b"), AX.X))
                done("bmask", dve.reduce_sum(bmask[:, :], rows, AX.X))
                after("bmask")
                done("pick", dve.tensor_copy(pick_b[:, :, :], bc(bmask[:, :].unsqueeze(2), B * E, B, P)))
                dve.wait_ge(made, 4)
                done("tok_row", dve.tensor_copy(tok_row[:, :], row_i[:, :]))
                done("tok_col", dve.tensor_copy(tok_col[:, :], col_i[:, :]))
                for t in range(NT):
                    if t % 4 == 0:
                        dve.wait_ge(load_x[t // 4], 16)
                    done(f"st{t}", dve.bn_stats(stats[:, t, :], x_in[:, t, :]))
                after(f"st{NT - 1}")
                for t in range(NT):
                    done(f"mv{t}", dve.bn_aggr(mv[:, t, :], stats[:, t, :]))
                after(f"mv{NT - 1}")
                done("var", dve.tensor_scalar(var[:, :], mv[:, :, 1], LN_EPS, None, ALU.add))
                dve.wait_ge(load_s, 64)
                done("cross_c", dve.tensor_scalar(cross_c[:, :], gain_in[:, :], 1.0 / (UNIT * UNIT), None, ALU.mult))
                done("score_c", dve.tensor_scalar(score_c[:, :], gain_in[:, :], 1.0 / (math.sqrt(P) * UNIT * UNIT), None,
                                                  ALU.mult))
                dve.wait_ge(a, act_at["rs"])
                done("nw1", dve.tensor_tensor(nw[:, :], rs[:, :], rs[:, :], ALU.mult))
                after("nw1")
                done("nw2", dve.tensor_tensor(nw[:, :], nw[:, :], var[:, :], ALU.mult))
                after("nw2")
                done("nw3", dve.tensor_scalar(nw[:, :], nw[:, :], -0.5, 1.5, ALU.mult, ALU.add))
                after("nw3")
                done("rstd", dve.tensor_tensor(rstd[:, :], rs[:, :], nw[:, :], ALU.mult))
                after("rstd")
                done("shift", dve.scalar_tensor_tensor(out=shift[:, :], in0=mv[:, :, 0], scalar=-1.0, in1=rstd[:, :],
                                                       op0=ALU.mult, op1=ALU.mult))
                for t in range(DVE_TILES):
                    done(f"xn{t}", dve.tensor_scalar(xn[:, t, :], x_in[:, t, :], mv[:, t, 0:1], rstd[:, t:t + 1],
                                                     ALU.subtract, ALU.mult))
                for w, name in enumerate("qk"):
                    for j in range(2):
                        dve.wait_ge(a, act_at[f"{name}{j}"])
                        cols = slice(j * GW, (j + 1) * GW)
                        done(f"{name}{j}", dve.tensor_tensor(proj_w[:, w, 1, cols], bank[2 + 2 * w + j][:, :],
                                                             proj_w[:, w, 0, cols].bitcast(fp32), ALU.subtract))
                for m in range(4):
                    dve.wait_ge(a, act_at[f"xT{m}"])
                    src = xT[:, m * 512:(m + 1) * 512].rearrange("p (b t) -> p b t", b=2)
                    hi, lo = xT_all[:, 2 * m:2 * m + 2, 0, :], xT_all[:, 2 * m:2 * m + 2, 1, :]
                    done(f"xTh{m}", dve.tensor_copy(hi, src))
                    after(f"xTh{m}")
                    done(f"xTl{m}", dve.tensor_tensor(lo, src, hi.bitcast(fp32), ALU.subtract))
                dve.wait_ge(pe_s, pe_at["logits"])
                lg = bank[2][:, 0:NT * (H + E)].rearrange("p (t c) -> p t c", t=NT)
                done("z", dve.tensor_tensor(z[:, :, :], lg[:, :, 0:H], bc(bg_in[:, :].unsqueeze(1), P, NT, H), ALU.add))
                after("z")
                done("zn", dve.tensor_scalar(zn[:, :, :], z[:, :, :], -1.0, 0.0, ALU.mult, ALU.max))
                after("zn")
                done("za", dve.scalar_tensor_tensor(out=za[:, :, :], in0=zn[:, :, :], scalar=2.0, in1=z[:, :, :],
                                                    op0=ALU.mult, op1=ALU.add))
                done("gmax", dve.tensor_reduce(gmax[:, :], lg[:, :, H:H + E], AX.X, ALU.max))
                after("gmax")
                done("gsh", dve.tensor_tensor(gsh[:, :, :], lg[:, :, H:H + E], bc(gmax[:, :].unsqueeze(2), P, NT, E),
                                              ALU.subtract))
                dve.wait_ge(a, act_at["zln"])
                done("logg", dve.tensor_tensor(logg[:, :, :], za[:, :, :], zn[:, :, :], ALU.add))
                dve.wait_ge(a, act_at["gexp"])
                done("gsum", dve.reduce_sum(gsum[:, :], gsh[:, :, :], AX.X))
                after("gsum")
                done("ginv", dve.reciprocal(ginv[:, :], gsum[:, :]))
                after("ginv")
                done("probs", dve.tensor_tensor(
                    probs[:, :, :, :].rearrange("p h b e -> p b h e"),
                    gsh[:, :, :].rearrange("p (b h) e -> p b h e", h=HT),
                    bc(ginv[:, :].rearrange("p (b h) -> p b h", h=HT).unsqueeze(3), P, B, HT, E), ALU.mult))
                for j in range(2):
                    dve.wait_ge(a, act_at[f"n{j}"])
                    cols = slice(j * GW, (j + 1) * GW)
                    done(f"n{j}", dve.tensor_tensor(proj_w[:, 2, 1, cols], bank[3 + j][:, :],
                                                    proj_w[:, 2, 0, cols].bitcast(fp32), ALU.subtract))
                dve.wait_ge(a, act_at["decay3"])
                flat = decay[:, :, :, :].rearrange("p b h k -> p (b h k)")
                done("decay", dve.tensor_scalar(flat, flat, cross_c[:, 0:1], None, ALU.mult))
                dve.wait_ge(pe_s, pe_at["probsT"])
                done("left", dve.tensor_copy(left[:, :], bank[6][0:B * E, 0:T]))
                assert n == len(steps)

        NB = 4
        FIND = 8
        with ExitStack() as c2:
            def sb2(name, shape, dt=fp32):
                return c2.enter_context(nc.sbuf_tensor(name, shape, dt))

            def sem2(name):
                return c2.enter_context(nc.semaphore(name))

            def sems2(name, n):
                return [sem2(f"{name}{i}") for i in range(n)]

            xs = sb2("xs", [P, 2, T], fp32r)
            top = sb2("top", [B * E, 2, K])
            top_i = sb2("top_i", [B * E, K], u32)
            best = sb2("best", [B * E, TOPS])
            best_i = sb2("best_i", [B * E, TOPS], u32)
            held = sb2("held", [B * E, 2])
            left_next = sb2("left_next", [B * E, T])
            top_t = sb2("top_t", [B * E, 2, K])
            qk = [sb2(f"qk{i}", [P, NB, GW]) for i in range(2)]
            junk = sb2("junk", [P, NB, G, P])
            ssq = [sb2(f"ssq{i}", [P, NB * G]) for i in range(2)]
            ms = sb2("ms", [P, NB * G])
            eps_c = sb2("eps_c", [P, NB * G])
            three_c = sb2("three_c", [P, NB * G])
            lms = sb2("lms", [P, NB * G])
            r0 = sb2("r0", [P, NB * G])
            nt = sb2("nt", [P, NB * G])
            vS = [sb2(f"vS{i}", [P, HT, GW]) for i in range(2)]
            qT = sb2("qT", [P, 2, G, T], fp16)
            kT = sb2("kT", [P, 2, G, T], fp16)
            sc = sb2("sc", [P, G * HT, C])
            ex = sb2("ex", [P, G * HT, C])
            smax = sb2("smax", [P, G * HT])
            ssum = sb2("ssum", [P, G * HT])
            sinv = sb2("sinv", [P, G * HT])
            AT = sb2("AT", [P, G, 3, P])

            s_zero = sem2("s_zero")
            xs_loaded = sem2("xs_loaded")
            experts_s = sem2("experts_loaded")
            pj = sems2("projected", 6)
            sq = sems2("squared", NB)
            raw = sems2("raw_copied", NB)
            vcp = sems2("v_copied", 2)
            mean = sems2("mean_sq", 2)
            lnm = sems2("ln_mean", 2)
            rsq = sems2("rsqrt", 2)
            newt = sem2("newton")
            nrm = sems2("normalised", 2)
            tr = sems2("transposed", NB)
            hi_s = sems2("hi_copied", NB)
            lo_s = sems2("lo_copied", NB)
            cross_s = sems2("cross_scores", 2)
            diag_s = sem2("chunk_scores")
            masked = sem2("masked")
            maxed = sem2("maxed")
            shifted = sem2("shifted")
            exped = sem2("exped")
            summed = sem2("summed")
            inverted = sem2("inverted")
            attn_s = sem2("attn_ready")
            ta = sem2("attn_turned")
            at_s = sem2("attn_T_copied")
            crossed = sems2("cross_weights", 2)
            av = sem2("weighted_values")
            summed_out = sem2("residual_added")
            topk = sem2("topk")
            slots = sem2("slots_turned")

            PJB = [bank[0], bank[1], bank[6]]
            TRB = [bank[2], bank[3]]
            DB, XB, OB = bank[4], bank[5], bank[7]

            block = c2.enter_context(nc.Block())

            @block.sync
            def _(sp):
                src = xT_all[:, :, :, :].bitcast(fp32).rearrange("p b c t -> p b (c t)")
                dst = xs[:, :, :].bitcast(fp32).rearrange("p c t -> p (c t)")
                sp.dma_start(dst, src[:, 2, :]).then_inc(xs_loaded, 16)
                sp.dma_start(w1_in[:, :, :], w1.rearrange("e d f -> d e f")).then_inc(experts_s, 16)
                sp.dma_start(w2_in[:, :, :], w2.rearrange("e (f p) d -> p (e f) d", p=P)).then_inc(experts_s, 16)
                with sp.Fori(3, B) as b:
                    sp.wait_ge(pj[5], 2 * b)
                    sp.dma_start(dst, src[:, ds(b, 1), :].rearrange("p o t -> p (o t)")).then_inc(xs_loaded, 16)
                sp.wait_ge(xs_loaded, 16 * (B - 2))
                sp.wait_ge(experts_s, 32)

            @block.tensor
            def _(pe):
                def project(b, g, k, fresh=False):
                    u = 2 * b + g
                    if isinstance(b, int) and b < 2:
                        x_T = xT_all[:, b, :, :]
                    else:
                        pe.wait_ge(xs_loaded, 16 * (b - 1))
                        x_T = xs[:, :, :]
                    tile, w = (k // 2, k % 2) if k < NB else (k - NB, 2)
                    if k >= 3:
                        pe.wait_ge(raw[k - 3], u + 1)
                    elif not fresh:
                        pe.wait_ge((raw[3], vcp[0], vcp[1])[k], u)
                    for n, (a_, b_) in enumerate(((1, 0), (0, 1), (0, 0))):
                        mm = pe.matmul(PJB[k % 3][:, :], x_T[:, a_, tile * P:(tile + 1) * P],
                                       proj_w[:, w, b_, g * GW:(g + 1) * GW], start=(n == 0), stop=(n == 2))
                    mm.then_inc(pj[k], 1)

                def turn(b, g, k, fresh=False):
                    u = 2 * b + g
                    pe.wait_ge(nrm[k // 2], u + 1)
                    if k >= 2:
                        pe.wait_ge(lo_s[k - 2], u + 1)
                    elif not fresh:
                        pe.wait_ge(lo_s[k + 2], u)
                    for h in range(G):
                        mm = pe.transpose(TRB[k % 2][:, h * P:(h + 1) * P], qk[g][:, k, h * P:(h + 1) * P], ident[:, :])
                    mm.then_inc(tr[k], 1)

                PARTS = ((1, 0), (0, 1), (0, 0))

                def cross(b, g, n, fresh=False):
                    u = 2 * b + g
                    if n == 0:
                        pe.wait_ge(lo_s[NB - 1], u + 1)
                        if not fresh:
                            pe.wait_ge(crossed[1], u)
                    else:
                        pe.wait_ge(crossed[0], u + 1)
                    for hh in range(2):
                        h, o = 2 * n + hh, hh * T
                        for m, (a_, b_) in enumerate(PARTS):
                            pe.matmul(XB[:, o:o + 3 * C], kT[:, a_, h, 0:P], qT[:, b_, h, C:T],
                                      start=(m == 0), stop=(m == 2))
                        for m, (a_, b_) in enumerate(PARTS):
                            mm = pe.matmul(XB[0:C, o + 3 * C:o + T], kT[:, a_, h, P:P + C], qT[:, b_, h, 3 * C:T],
                                           start=(m == 0), stop=(m == 2))
                    mm.then_inc(cross_s[n], 1)

                def chunk(b, g, fresh=False):
                    if not fresh:
                        pe.wait_ge(at_s, 2 * b + g)
                    for h in range(G):
                        for t in range(HT):
                            for c in range(2):
                                o = t * P + c * C
                                for m, (a_, b_) in enumerate(PARTS):
                                    mm = pe.matmul(DB[c * C:(c + 1) * C, (h * HT + t) * C:(h * HT + t + 1) * C],
                                                   qT[:, a_, h, o:o + C], kT[:, b_, h, o:o + C],
                                                   start=(m == 0), stop=(m == 2))
                    mm.then_inc(diag_s, 1)

                def turn_attn(b, g):
                    pe.wait_ge(attn_s, 2 * b + g + 1)
                    for h in range(G):
                        mm = pe.transpose(DB[:, h * P:(h + 1) * P], ex[:, h * HT:(h + 1) * HT, :].rearrange("p t s -> p (t s)"),
                                          ident[:, :])
                    mm.then_inc(ta, 1)

                def values(b, g, h, fresh=False):
                    u = 2 * b + g
                    if h == 0:
                        pe.wait_ge(at_s, u + 1)
                        pe.wait_ge(crossed[1], u + 1)
                        pe.wait_ge(vcp[1], u + 1)
                        if g == 0 and not fresh:
                            pe.wait_ge(summed_out, b)
                    for n, (blk, src, dst) in enumerate(((0, 0, 0), (2, 0, 1), (1, 1, 1))):
                        mm = pe.matmul(OB[:, dst * D:(dst + 1) * D], AT[:, h, blk, :],
                                       vS[g][:, src, h * P:(h + 1) * P], start=(g == 0 and h == 0 and n == 0),
                                       stop=(g == 1 and h == G - 1 and n > 0), skip_group_check=True)
                    if h == G - 1:
                        mm.then_inc(av, 1)

                def step(b, g, first=False, last=False, fresh1=False):
                    nb, ng = (b, 1) if g == 0 else (b + 1, 0)
                    pb, pg = (b, 0) if g == 1 else (b - 1, 1)
                    turn(b, g, 0, first)
                    if not last:
                        project(nb, ng, 0)
                    turn(b, g, 1, first)
                    if not last:
                        project(nb, ng, 1)
                    turn(b, g, 2)
                    if not last:
                        project(nb, ng, 2)
                    if not first:
                        turn_attn(pb, pg)
                    turn(b, g, 3)
                    if not last:
                        project(nb, ng, 3)
                        project(nb, ng, 4)
                    if not first:
                        for h in range(G):
                            values(pb, pg, h, fresh1)
                    if not last:
                        project(nb, ng, 5)
                    cross(b, g, 0, first)
                    chunk(b, g, first)
                    cross(b, g, 1)

                for k in range(6):
                    project(0, 0, k, fresh=True)
                step(0, 0, first=True)
                step(0, 1, fresh1=True)
                step(1, 0)
                with pe.Fori(1, B - 1) as j:
                    step(j, 1)
                    step(j + 1, 0)
                step(B - 1, 1, last=True)
                pe.wait_ge(topk, FIND * (K // TOPS) + 2)
                pe.transpose(bank[0][:, 0:B * E], top[:, :, :].rearrange("p a k -> p (a k)"), ident[0:B * E, 0:B * E])
                pe.transpose(bank[0][:, 64:64 + B * E], top_t[:, :, :].rearrange("p a k -> p (a k)"),
                             ident[0:B * E, 0:B * E]).then_inc(slots, 1)
                turn_attn(B - 1, 1)
                for h in range(G):
                    values(B - 1, 1, h)

            @block.scalar
            def _(act):
                def square(b, g, k, fresh=False):
                    u = 2 * b + g
                    act.wait_ge(pj[k], u + 1)
                    if not fresh:
                        act.wait_ge(sq[k], u)
                        act.wait_ge(nrm[k // 2], u - 1)
                    for h in range(G):
                        ins = act.activation(junk[:, k, h, :], PJB[k % 3][:, h * P:(h + 1) * P], ACT.Square,
                                             accum_out=ssq[g][:, k * G + h:k * G + h + 1])
                    ins.then_inc(sq[k], 1)

                def rsqrt(b, g, t):
                    u = 2 * b + g
                    cols = slice(t * 2 * G, (t + 1) * 2 * G)
                    act.wait_ge(mean[t], u + 1)
                    act.activation(lms[:, cols], ms[:, cols], ACT.Ln, scale=1.0 / P).then_inc(lnm[t], 1)
                    act.wait_ge(lnm[t], u + 1)
                    act.activation(r0[:, cols], lms[:, cols], ACT.Exp, scale=-0.5).then_inc(rsq[t], 1)

                def hi(b, g, k):
                    dst = (qT, kT)[k % 2][:, 0, :, (k // 2) * P:(k // 2 + 1) * P]
                    act.wait_ge(tr[k], 2 * b + g + 1)
                    act.activation(dst, TRB[k % 2][:, :].rearrange("p (h t) -> p h t", h=G), ACT.Copy)\
                       .then_inc(hi_s[k], 1)

                def value(b, g, t, fresh=False):
                    u = 2 * b + g
                    act.wait_ge(pj[NB + t], u + 1)
                    if not fresh:
                        act.wait_ge(av, u - 1)
                    act.activation(vS[g][:, t, :], PJB[1 + t][:, :], ACT.Copy).then_inc(vcp[t], 1)

                def exps(b, g):
                    act.wait_ge(shifted, 2 * b + g + 1)
                    act.activation(ex[:, :, :], sc[:, :, :], ACT.Exp).then_inc(exped, 1)

                def attn_T(b, g):
                    act.wait_ge(ta, 2 * b + g + 1)
                    for t in range(HT):
                        for c in range(2):
                            rows = slice(c * C, (c + 1) * C)
                            ins = act.activation(AT[rows, :, t, rows],
                                                 DB[t * C:(t + 1) * C, :].rearrange("p (h c) -> p h c", h=G)[:, :, rows],
                                                 ACT.Copy)
                    ins.then_inc(at_s, 1)

                def step(b, g, first=False, last=False, fresh=False):
                    nb, ng = (b, 1) if g == 0 else (b + 1, 0)
                    pb, pg = (b, 0) if g == 1 else (b - 1, 1)
                    hi(b, g, 0)
                    if not first:
                        exps(pb, pg)
                    if not last:
                        square(nb, ng, 0, fresh)
                    hi(b, g, 1)
                    if not last:
                        square(nb, ng, 1, fresh)
                        rsqrt(nb, ng, 0)
                    if not first:
                        attn_T(pb, pg)
                    hi(b, g, 2)
                    hi(b, g, 3)
                    if not last:
                        square(nb, ng, 2, fresh)
                        square(nb, ng, 3, fresh)
                        value(nb, ng, 0, fresh)
                        rsqrt(nb, ng, 1)
                        value(nb, ng, 1, fresh)

                act.preload_act_table_set("natural_log_exp_and_others")
                act.wait_ge(s_zero, 4)
                for k in range(NB):
                    square(0, 0, k, fresh=True)
                    if k % 2:
                        rsqrt(0, 0, k // 2)
                for t in range(HT):
                    value(0, 0, t, fresh=True)
                step(0, 0, first=True, fresh=True)
                step(0, 1)
                step(1, 0)
                with act.Fori(1, B - 1) as j:
                    step(j, 1)
                    step(j + 1, 0)
                step(B - 1, 1, last=True)
                exps(B - 1, 1)
                attn_T(B - 1, 1)

            @block.gpsimd
            def _(pool):
                pool.memset(AT[:, :, :, :], 0.0).then_inc(s_zero, 1)
                pool.memset(junk[:, :, :, :], 0.0).then_inc(s_zero, 1)
                pool.memset(eps_c[:, :], P * RMS_EPS).then_inc(s_zero, 1)
                pool.memset(three_c[:, :], 3.0 * P).then_inc(s_zero, 1)
                pool.wait_ge(s_zero, 4)

                def normalise(b, g, t):
                    u = 2 * b + g
                    cols = slice(t * 2 * G, (t + 1) * 2 * G)
                    pool.wait_ge(sq[2 * t + 1], u + 1)
                    pool.tensor_tensor(ms[:, cols], ssq[g][:, cols], eps_c[:, cols], ALU.add).then_inc(mean[t], 1)
                    n0 = 8 * u + 4 * t
                    pool.wait_ge(rsq[t], u + 1)
                    pool.tensor_tensor(nt[:, cols], r0[:, cols], r0[:, cols], ALU.mult).then_inc(newt, 1)
                    pool.wait_ge(newt, n0 + 1)
                    pool.tensor_tensor(nt[:, cols], nt[:, cols], ms[:, cols], ALU.mult).then_inc(newt, 1)
                    pool.wait_ge(newt, n0 + 2)
                    pool.tensor_tensor(nt[:, cols], three_c[:, cols], nt[:, cols], ALU.subtract).then_inc(newt, 1)
                    pool.wait_ge(newt, n0 + 3)
                    pool.tensor_tensor(nt[:, cols], nt[:, cols], r0[:, cols], ALU.mult).then_inc(newt, 1)
                    pool.wait_ge(newt, n0 + 4)
                    pool.wait_ge(raw[2 * t + 1], u + 1)
                    rows = qk[g][:, 2 * t:2 * t + 2, :].rearrange("p k (h d) -> p (k h) d", h=G)
                    pool.tensor_tensor(rows, rows, bc(nt[:, cols].unsqueeze(2), P, 2 * G, P), ALU.mult)\
                        .then_inc(nrm[t], 1)

                with pool.Fori(0, B) as b:
                    for g in range(2):
                        for t in range(HT):
                            normalise(b, g, t)

            @block.vector
            def _(dve):
                def raw_copy(b, g, k):
                    dve.wait_ge(sq[k], 2 * b + g + 1)
                    dve.tensor_copy(qk[g][:, k, :], PJB[k % 3][:, :]).then_inc(raw[k], 1)

                def lo(b, g, k):
                    cols = slice((k // 2) * P, (k // 2 + 1) * P)
                    w = (qT, kT)[k % 2]
                    dve.wait_ge(hi_s[k], 2 * b + g + 1)
                    dve.tensor_tensor(w[:, 1, :, cols], TRB[k % 2][:, :].rearrange("p (h t) -> p h t", h=G),
                                      w[:, 0, :, cols], ALU.subtract).then_inc(lo_s[k], 1)

                def softmax_shift(b, g):
                    u = 2 * b + g
                    dve.wait_ge(diag_s, u + 1)
                    dve.scalar_tensor_tensor(out=sc[:, :, :], in0=DB[:, :].rearrange("p (h s) -> p h s", s=C),
                                             scalar=score_c[:, 0:1], in1=bc(causal[:, :].unsqueeze(1), P, G * HT, C),
                                             op0=ALU.mult, op1=ALU.add).then_inc(masked, 1)
                    dve.wait_ge(masked, u + 1)
                    dve.tensor_reduce(smax[:, :], sc[:, :, :], AX.X, ALU.max).then_inc(maxed, 1)
                    dve.wait_ge(maxed, u + 1)
                    dve.tensor_tensor(sc[:, :, :], sc[:, :, :], bc(smax[:, :].unsqueeze(2), P, G * HT, C),
                                      ALU.subtract).then_inc(shifted, 1)

                def softmax_norm(b, g):
                    u = 2 * b + g
                    dve.wait_ge(exped, u + 1)
                    dve.reduce_sum(ssum[:, :], ex[:, :, :], AX.X).then_inc(summed, 1)
                    dve.wait_ge(summed, u + 1)
                    dve.reciprocal(sinv[:, :], ssum[:, :]).then_inc(inverted, 1)
                    dve.wait_ge(inverted, u + 1)
                    dve.tensor_tensor(ex[:, :, :], ex[:, :, :], bc(sinv[:, :].unsqueeze(2), P, G * HT, C), ALU.mult)\
                       .then_inc(attn_s, 1)

                def cross_weights(b, g, n):
                    dve.wait_ge(cross_s[n], 2 * b + g + 1)
                    src = XB[:, :].rearrange("p (h t) -> p h t", h=2)
                    heads = slice(2 * n, 2 * n + 2)
                    ends = XB[0:C, :].rearrange("p (h k t) -> p h k t", h=2, t=C)[:, :, 0:4:3, :]
                    dve.tensor_scalar(AT[0:C, heads, 0:2, C:P], ends, cross_c[0:C, 0:1], None, ALU.mult)
                    w = decay[:, ds(b, 1), g * G + 2 * n:g * G + 2 * n + 2, :].rearrange("p o h k -> p (o h) k")
                    dve.tensor_tensor(AT[:, heads, 2, :].rearrange("p h (k t) -> p h k t", k=2),
                                      src[:, :, C:3 * C].rearrange("p h (k t) -> p h k t", k=2),
                                      bc(w.unsqueeze(3), P, 2, 2, C), ALU.mult).then_inc(crossed[n], 1)

                def residual(b):
                    dve.wait_ge(av, 2 * b + 2)
                    rows = x_in[:, ds(HT * b, HT), :].rearrange("p h d -> p (h d)")
                    dve.tensor_tensor(rows, rows, OB[:, 0:T], ALU.add).then_inc(summed_out, 1)

                def find(r):
                    if not isinstance(r, int) or r:
                        dve.wait_ge(topk, FIND * r - 3)
                        dve.tensor_copy(top[:, 0, ds((r - 1) * TOPS, TOPS)], best[:, :]).then_inc(topk, 1)
                        dve.tensor_copy(top_i[:, ds((r - 1) * TOPS, TOPS)], best_i[:, :]).then_inc(topk, 1)
                        dve.tensor_copy(left[:, :], left_next[:, :]).then_inc(topk, 1)
                        dve.wait_ge(topk, FIND * r)
                    dve.tensor_copy(held[:, 0:1], left[:, 0:1]).then_inc(topk, 1)
                    dve.max(best[:, :], left[:, :]).then_inc(topk, 1)
                    dve.wait_ge(topk, FIND * r + 2)
                    dve.tensor_copy(held[:, 1:2], best[:, 0:1]).then_inc(topk, 1)
                    dve.max_index(best_i[:, :], best[:, :], left[:, :]).then_inc(topk, 1)
                    dve.match_replace(left_next[:, :], best[:, :], left[:, :], -1.0).then_inc(topk, 1)

                def tokens_of_slots():
                    done = FIND * (K // TOPS)
                    dve.wait_ge(topk, done - 3)
                    dve.tensor_copy(top[:, 0, (K // TOPS - 1) * TOPS:], best[:, :]).then_inc(topk, 1)
                    dve.tensor_copy(top_i[:, (K // TOPS - 1) * TOPS:], best_i[:, :]).then_inc(topk, 1)
                    dve.wait_ge(topk, done - 1)
                    dve.tensor_copy(top[:, 1, :], top[:, 0, :]).then_inc(topk, 1)
                    dve.tensor_copy(top_t[:, 0, :], top_i[:, :]).then_inc(topk, 1)
                    dve.tensor_copy(top_t[:, 1, :], top_i[:, :]).then_inc(topk, 1)
                    dve.wait_ge(topk, done + 2)
                    dve.tensor_tensor(
                        tok_spread[:, :].rearrange("p (e k) -> p e k", e=E), bc(top_t[:, 0, :].unsqueeze(1), B * E, E, K),
                        bc(emask[:, :].unsqueeze(2), B * E, E, K), ALU.mult).then_inc(topk, 1)

                def slot_rows():
                    dve.wait_ge(slots, 1)
                    for dst, at in ((slot_gate, 0), (slot_tok, 64)):
                        for odd in range(2):
                            rows = slice(odd * K, (odd + 1) * K)
                            src = bank[0][rows, at:at + B * E].rearrange("p (bp o e) -> p o e bp", o=2, e=E)[:, odd]
                            dve.tensor_scalar(dst[rows, :, :], src, float(T * odd * (at > 0)), None, ALU.add)

                def step(b, g, first=False, last=False):
                    nb, ng = (b, 1) if g == 0 else (b + 1, 0)
                    pb, pg = (b, 0) if g == 1 else (b - 1, 1)
                    if not first:
                        softmax_shift(pb, pg)
                    lo(b, g, 0)
                    if not first:
                        softmax_norm(pb, pg)
                    lo(b, g, 1)
                    if not last:
                        raw_copy(nb, ng, 0)
                    if not last:
                        raw_copy(nb, ng, 1)
                    if not first:
                        cross_weights(pb, pg, 1)
                    lo(b, g, 2)
                    lo(b, g, 3)
                    if not last:
                        raw_copy(nb, ng, 2)
                        raw_copy(nb, ng, 3)
                    if g == 1:
                        find(b)
                    if g == 0 and not first:
                        residual(pb)
                    if last:
                        tokens_of_slots()
                    cross_weights(b, g, 0)

                dve.wait_ge(s_zero, 4)
                for k in range(NB):
                    raw_copy(0, 0, k)
                step(0, 0, first=True)
                step(0, 1)
                step(1, 0)
                with dve.Fori(1, B - 1) as j:
                    step(j, 1)
                    step(j + 1, 0)
                step(B - 1, 1, last=True)
                softmax_shift(B - 1, 1)
                cross_weights(B - 1, 1, 1)
                softmax_norm(B - 1, 1)
                slot_rows()
                residual(B - 1)

        front.close()

        with ExitStack() as c3:
            def sb3(name, shape, dt=fp32):
                return c3.enter_context(nc.sbuf_tensor(name, shape, dt))

            def sem3(name):
                return c3.enter_context(nc.semaphore(name))

            def sems3(name, n):
                return [sem3(f"{name}{i}") for i in range(n)]

            NSLOT = B * K
            onehot = [sb3(f"onehot{i}", [P, HT, E * K], fp16) for i in range(2)]
            picked = sb3("picked", [P, 2, E, NSLOT], fp32r)
            tok_bc = [sb3(f"tok_bc{i}", [P, E * K], fp16) for i in range(2)]
            w1_hl = [sb3(f"w1_hl{i}", [P, 2, F], fp32r) for i in range(2)]
            hid = [sb3(f"hid{i}", [P, FT, NSLOT]) for i in range(2)]
            back = [sb3(f"back{i}", [P, BP, 2 * T], fp32r) for i in range(2)]
            y = [sb3(f"y{i}", [P, BP, D]) for i in range(2)]
            y_hl = [sb3(f"y_hl{i}", [P, 2, BP, D], fp32r) for i in range(2)]
            moe = sb3("moe", [P, NT * P], bf16)

            asked = sem3("tokens_spread")
            spread = sem3("tokens_copied")
            hot = sem3("onehots")
            gath = sem3("gathered")
            gath_h = sem3("gathered_hi")
            gath_l = sem3("gathered_lo")
            w1h_s = sems3("w1_hi", 2)
            w1l_s = sems3("w1_lo", 2)
            up = sems3("up_done", FT)
            gelu = sems3("gelu_done", FT)
            down = sem3("down_done")
            gated = sem3("gated")
            y_hi = sem3("y_hi")
            y_lo = sem3("y_lo")
            back_s = sem3("scatter_ready")
            scat = sem3("scattered")
            moe_s = sem3("moe_rounded")
            moe_t = sem3("moe_turned")
            res_s = sem3("summed_up")
            out_s = sem3("stored")

            ACC = bank[0:4]
            UPB = [bank[4], bank[5]]
            YB = [bank[6], bank[7]]
            block = c3.enter_context(nc.Block())
            out_v = out.rearrange("b (h p) d -> p (b h) d", p=P)

            @block.sync
            def _(sp):
                for m in range(4):
                    sp.wait_ge(res_s, m + 1)
                    sp.dma_start(out_v[:, 4 * m:4 * m + 4, :], x_in[:, 4 * m:4 * m + 4, :]).then_inc(out_s, 16)
                sp.wait_ge(out_s, 64)

            @block.tensor
            def _(pe):
                def ask(j, k, first=False):
                    if not first:
                        pe.wait_ge(spread, 2 * j + k - 1)
                    pe.matmul(bank[k][:, :], pick_b[:, ds(2 * j + k, 1), :].rearrange("p o t -> p (o t)"),
                              tok_spread[:, :], start=True, stop=True).then_inc(asked, 1)

                def gather(j, k, first=False):
                    b = 2 * j + k
                    pe.wait_ge(hot, b + 1)
                    if not first:
                        pe.wait_ge(gath_l, b - 1)
                    for n, (rows, t) in enumerate(((xn_l, 0), (xn_l, 1), (xn_h, 0), (xn_h, 1))):
                        mm = pe.matmul(bank[2 + k][:, :], rows[:, ds(HT * b + t, 1), :].rearrange("p o d -> p (o d)"),
                                       onehot[k][:, t, :], start=(n == 0), stop=(n == 3))
                    mm.then_inc(gath, 1)

                ask(0, 0, first=True)
                ask(0, 1, first=True)
                for k in range(2):
                    ask(1, k)
                    gather(0, k, first=True)
                with pe.Fori(1, B // 2 - 1) as j:
                    for k in range(2):
                        ask(j + 1, k)
                        gather(j, k)
                for k in range(2):
                    gather(B // 2 - 1, k)
                pe.wait_ge(gath_l, B)

                def ups(e, par, j):
                    pe.wait_ge(w1l_s[par], j + 1)
                    for f in range(FT):
                        if f >= 2:
                            pe.wait_ge(gelu[f - 2], e + 1)
                        elif not isinstance(e, int) or e:
                            pe.wait_ge(gelu[f + 2], e)
                        for n, (a_, b_) in enumerate(((1, 0), (0, 1), (0, 0))):
                            mm = pe.matmul(UPB[f % 2][:, :], w1_hl[par][:, a_, f * P:(f + 1) * P],
                                           picked[:, b_, ds(e, 1), :].rearrange("p o s -> p (o s)"),
                                           start=(n == 0), stop=(n == 2))
                        mm.then_inc(up[f], 1)

                def downs(e, par, j):
                    pe.wait_ge(gelu[FT - 1], e + 1)
                    if not isinstance(e, int) or e >= 2:
                        pe.wait_ge(gated, e - 1)
                    for s in range(BP):
                        for f in range(FT):
                            mm = pe.matmul(YB[par][:, s * D:(s + 1) * D], hid[par][:, f, s * P:(s + 1) * P],
                                           w2_in[:, ds(FT * e + f, 1), :].rearrange("p o d -> p (o d)"), start=(f == 0), stop=(f == FT - 1))
                    mm.then_inc(down, 1)

                def scatter(e, par, first=False):
                    pe.wait_ge(y_lo, e + 1)
                    pe.wait_ge(back_s, BP * e + BP)
                    for s in range(BP):
                        for n in (1, 0):
                            mm = pe.matmul(ACC[s][:, :], y_hl[par][:, n, s, :], back[par][:, s, :],
                                           start=(first and n == 1), stop=True, skip_group_check=True)
                    mm.then_inc(scat, 1)

                ups(0, 0, 0)
                ups(1, 1, 0)
                downs(0, 0, 0)
                ups(2, 0, 1)
                scatter(0, 0, first=True)
                downs(1, 1, 0)
                ups(3, 1, 1)
                scatter(1, 1)
                downs(2, 0, 1)
                with pe.Fori(2, E // 2) as j:
                    ups(2 * j, 0, j)
                    scatter(2 * j - 2, 0)
                    downs(2 * j - 1, 1, j - 1)
                    ups(2 * j + 1, 1, j)
                    scatter(2 * j - 1, 1)
                    downs(2 * j, 0, j)
                scatter(E - 2, 0)
                downs(E - 1, 1, E // 2 - 1)
                scatter(E - 1, 1)
                for m in range(4):
                    pe.wait_ge(moe_s, m + 1)
                    for t in range(4):
                        mm = pe.transpose(bank[4 + m][:, :].bitcast(bf16)[:, t * P:(t + 1) * P],
                                          moe[:, (4 * m + t) * P:(4 * m + t + 1) * P], ident_b[:, :])
                    mm.then_inc(moe_t, 1)

            @block.scalar
            def _(act):
                def copy_tokens(j, k, first=False):
                    act.wait_ge(asked, 2 * j + k + 1)
                    if not first:
                        act.wait_ge(hot, 2 * j + k - 1)
                    act.activation(tok_bc[k][:, :], bank[k][:, :], ACT.Copy).then_inc(spread, 1)

                def gathered_hi(j, k):
                    b = 2 * j + k
                    act.wait_ge(gath, b + 1)
                    act.activation(picked[:, 0, :, ds(K * b, K)], bank[2 + k][:, :].rearrange("p (e s) -> p e s", e=E),
                                   ACT.Copy).then_inc(gath_h, 1)

                for k in range(2):
                    copy_tokens(0, k, first=True)
                with act.Fori(0, B // 2 - 1) as j:
                    for k in range(2):
                        copy_tokens(j + 1, k)
                        gathered_hi(j, k)
                for k in range(2):
                    gathered_hi(B // 2 - 1, k)

                def gelus(j, first=False):
                    for par in range(2):
                        e = 2 * j + par
                        for f in range(FT):
                            act.wait_ge(up[f], e + 1)
                            if f == 0 and not first:
                                act.wait_ge(down, e - 1)
                            act.activation(hid[par][:, f, :], UPB[f % 2][:, :], ACT.Gelu_apprx_tanh)\
                               .then_inc(gelu[f], 1)

                gelus(0, first=True)
                with act.Fori(1, E // 2) as j:
                    gelus(j)
                act.wait_ge(scat, E)
                for m in range(4):
                    act.activation(moe[:, m * 512:(m + 1) * 512], ACC[m][:, :], ACT.Copy).then_inc(moe_s, 1)

            @block.gpsimd
            def _(pool):
                for e in range(2):
                    pool.tensor_copy(w1_hl[e][:, 0, :], w1_in[:, e, :]).then_inc(w1h_s[e], 1)
                    pool.wait_ge(w1h_s[e], 1)
                    pool.tensor_tensor(w1_hl[e][:, 1, :], w1_in[:, e, :], w1_hl[e][:, 0, :].bitcast(fp32),
                                       ALU.subtract).then_inc(w1l_s[e], 1)

            @block.vector
            def _(dve):
                def split_w1(par, j):
                    dve.wait_ge(up[FT - 1], 2 * j + par - 1)
                    src = w1_in[:, ds(2 * j + par, 1), :].rearrange("p o f -> p (o f)")
                    dve.tensor_copy(w1_hl[par][:, 0, :], src).then_inc(w1h_s[par], 1)
                    dve.wait_ge(w1h_s[par], j + 1)
                    dve.tensor_tensor(w1_hl[par][:, 1, :], src, w1_hl[par][:, 0, :].bitcast(fp32),
                                      ALU.subtract).then_inc(w1l_s[par], 1)

                def onehots(j, k, first=False):
                    b = 2 * j + k
                    dve.wait_ge(spread, b + 1)
                    if not first:
                        dve.wait_ge(gath, b - 1)
                    for t in range(HT):
                        ins = dve.tensor_scalar(onehot[k][:, t, :], tok_bc[k][:, :], tok_col[:, t:t + 1], None,
                                                ALU.is_equal)
                    ins.then_inc(hot, 1)

                def gathered_lo(j, k):
                    b = 2 * j + k
                    dve.wait_ge(gath_h, b + 1)
                    dve.tensor_tensor(picked[:, 1, :, ds(K * b, K)],
                                      bank[2 + k][:, :].rearrange("p (e s) -> p e s", e=E),
                                      picked[:, 0, :, ds(K * b, K)].bitcast(fp32), ALU.subtract).then_inc(gath_l, 1)

                for k in range(2):
                    onehots(0, k, first=True)
                with dve.Fori(0, B // 2 - 1) as j:
                    for k in range(2):
                        onehots(j + 1, k)
                        gathered_lo(j, k)
                for k in range(2):
                    gathered_lo(B // 2 - 1, k)

                def expert(e, par, j, peel=False, last=False):
                    for s in range(BP):
                        if s == 0 and not peel:
                            dve.wait_ge(scat, e - 1)
                        dve.tensor_scalar(back[par][:, s, :], tok_row[:, :],
                                          slot_tok[:, ds(e, 1), s:s + 1].rearrange("p o k -> p (o k)"), None,
                                          ALU.is_equal).then_inc(back_s, 1)
                    if not last:
                        split_w1(par, j + 1)
                    dve.wait_ge(down, e + 1)
                    dve.tensor_tensor(y[par][:, :, :], YB[par][:, :].rearrange("p (s d) -> p s d", s=BP),
                                      bc(slot_gate[:, ds(e, 1), :].rearrange("p o s -> p (o s)").unsqueeze(2), P, BP, D),
                                      ALU.mult).then_inc(gated, 1)
                    dve.wait_ge(gated, e + 1)
                    dve.tensor_copy(y_hl[par][:, 0, :, :], y[par][:, :, :]).then_inc(y_hi, 1)
                    dve.wait_ge(y_hi, e + 1)
                    dve.tensor_tensor(y_hl[par][:, 1, :, :], y[par][:, :, :], y_hl[par][:, 0, :, :].bitcast(fp32),
                                      ALU.subtract).then_inc(y_lo, 1)

                for par in range(2):
                    expert(par, par, 0, peel=True)
                with dve.Fori(1, E // 2 - 1) as j:
                    for par in range(2):
                        expert(2 * j + par, par, j)
                for par in range(2):
                    expert(E - 2 + par, par, E // 2 - 1, last=True)
                for m in range(4):
                    dve.wait_ge(moe_t, m + 1)
                    dve.tensor_tensor(x_in[:, 4 * m:4 * m + 4, :], x_in[:, 4 * m:4 * m + 4, :],
                                      bank[4 + m][:, :].bitcast(bf16)[:, 0:512].rearrange("p (t d) -> p t d", t=4),
                                      ALU.add).then_inc(res_s, 1)


_INS = ['L0_attn_x', 'L0_attn_Wq', 'L0_attn_Wk', 'L0_attn_Wv', 'L0_attn_Wg', 'L0_attn_bg', 'L0_attn_Wo',
        'L0_attn_qk_gain', 'L0_ffn_gate_w', 'L0_ffn_w1', 'L0_ffn_w2']
_OUTS = [((8, 256, 128), 'float32')]


def kernel(**inputs):
    import numpy as _np
    import concourse.bacc as _bacc
    from concourse import mybir as _mybir
    from concourse.bass_utils import run_bass_kernel_spmd as _run

    nc = _bacc.Bacc("TRN2", target_bir_lowering=False, num_devices=1)
    arrays, args = {}, []
    for name in _INS:
        a = _np.ascontiguousarray(inputs[name])
        if name == 'L0_attn_qk_gain':
            a = a.reshape(1)
        arrays[f"in_{name}_dram"] = a
        args.append(nc.dram_tensor(f"in_{name}_dram", a.shape, _mybir.dt.from_np(a.dtype), kind="ExternalInput").ap())
    for i, (shape, dtype) in enumerate(_OUTS):
        dt = _mybir.dt.from_np(_np.dtype(dtype))
        args.append(nc.dram_tensor(f"out_{i}_dram", shape, dt, kind="ExternalOutput").ap())
    norm_attention_and_expert_choice_ffn_kernel(nc, *args)
    r = _run(nc, [arrays], core_ids=[0])
    got = tuple(r.results[0][f"out_{i}_dram"] for i in range(len(_OUTS)))
    return got[0]
```

```python
import math
import concourse.bass as bass
from concourse import mybir
from contextlib import ExitStack


def norm_attention_and_expert_choice_ffn_kernel(
    nc: bass.Bass,
    x: bass.AP,
    Wq: bass.AP,
    Wk: bass.AP,
    Wv: bass.AP,
    Wg: bass.AP,
    bg: bass.AP,
    Wo: bass.AP,
    qk_gain: bass.AP,
    gate_w: bass.AP,
    w1: bass.AP,
    w2: bass.AP,
    out: bass.AP,
):
    fp32 = mybir.dt.float32
    fp32r = mybir.dt.float32r
    fp16 = mybir.dt.float16
    bf16 = mybir.dt.bfloat16
    i32 = mybir.dt.int32
    u32 = mybir.dt.uint32
    ALU = mybir.AluOpType
    ACT = mybir.ActivationFunctionType
    AX = mybir.AxisListType
    ds = bass.ds

    P = 128
    B, T, D = x.shape
    HT = T // P
    NT = B * HT
    H = Wg.shape[0]
    C = 64
    G = 4
    GW = G * P
    E = gate_w.shape[1]
    F = w1.shape[2]
    FT = F // P
    K = 2 * T // E
    BP = B * K // P
    TOPS = 8
    LN_EPS, RMS_EPS = 1e-5, 1e-6
    NEG = -1.0e30
    TINY = 1.0e-15
    UNIT = 2.0 * P
    assert D == P and HT == 2 and T == 4 * C and H == 2 * G and 2 * K == P and B * E == 64 and E == H
    assert B == 8

    def bc(ap, *shape):
        return ap.broadcast_to(list(shape))

    ctx = ExitStack()
    with ctx:
        def sb(name, shape, dt=fp32):
            return ctx.enter_context(nc.sbuf_tensor(name, shape, dt))

        def sem(name):
            return ctx.enter_context(nc.semaphore(name))

        def sems(name, n):
            return [sem(f"{name}{i}") for i in range(n)]

        bank = [ctx.enter_context(nc.psum_tensor(f"bank{i}", [P, 512], fp32)) for i in range(8)]

        x_in = sb("x_in", [P, NT, D])
        xn_h = sb("xn_h", [P, NT, D], fp16)
        xn_l = sb("xn_l", [P, NT, D], fp16)
        decay = sb("decay", [P, B, H, 2])
        score_c = sb("score_c", [P, 1])
        cross_c = sb("cross_c", [P, 1])
        causal_b = sb("causal_b", [P, G * HT, C], bf16)
        ident = sb("ident", [P, P])
        ident_b = sb("ident_b", [P, P], bf16)
        slot_gate = sb("slot_gate", [P, E, BP])
        slot_tok = sb("slot_tok", [P, E, BP])
        tok_spread = sb("tok_spread", [B * E, E * K], fp16)
        pick_b = sb("pick_b", [B * E, B, P], fp16)
        tok_col = sb("tok_col", [P, HT])
        tok_row = sb("tok_row", [P, HT * T])
        w1_in = sb("w1_in", [P, E, F])
        w2_in = sb("w2_in", [P, E * FT, D])
        place = w1_in[:, :, :].rearrange("p e f -> p (e f)")
        xT = place[:, 0:NT * P]
        wv_in = place[:, NT * P:NT * P + H * D].rearrange("p (h d) -> p h d", h=H)
        wo_T = place[:, NT * P + H * D:NT * P + 2 * H * D].rearrange("p (h d) -> p h d", h=H)
        xn = sb("xn", [P, NT, D])
        gates_w = sb("gates_w", [P, H + E])
        bg_in = sb("bg_in", [P, H])
        later = sb("later", [P, P])
        whole = sb("whole", [P, P])
        w1_hl = [sb(f"w1_hl{i}", [P, 2, F], fp32r) for i in range(2)]
        w1h_s = sems("w1_hi", 2)
        w1l_s = sems("w1_lo", 2)
        xT_all = sb("xT_all", [P, B, 2, T], fp32r)
        proj_w = sb("proj_w", [P, 3, 2, H * P], fp32r)
        left = sb("left", [B * E, T])
        emask = sb("emask", [B * E, E])
        bmask = sb("bmask", [B * E, B])
        row_i = sb("row_i", [P, HT * T], i32)
        col_i = sb("col_i", [P, HT], i32)
        NSLOT = B * K
        picked = [xT_all[:, :, :, :].rearrange("p b c t -> p (b c t)")[:, 0:E * NSLOT],
                  proj_w[:, :, :, :].rearrange("p w c n -> p (w c n)")[:, 0:E * NSLOT]]
        picked = [part.rearrange("p (e s) -> p e s", e=E) for part in picked]

        AT = sb("AT", [P, G, 3, P])

        with ExitStack() as c1:
            def sb1(name, shape, dt=fp32):
                return c1.enter_context(nc.sbuf_tensor(name, shape, dt))

            def sem1(name):
                return c1.enter_context(nc.semaphore(name))

            wq_in = sb1("wq_in", [P, H, D])
            wk_in = sb1("wk_in", [P, H, D])
            wo_in = sb1("wo_in", [P, H * P])
            gain_in = sb1("gain_in", [P, 1])
            sign = sb1("sign", [P, 1])
            gain_abs = sb1("gain_abs", [P, 1])
            causal = sb1("causal", [P, C])
            stats = sb1("stats", [P, NT, 6])
            mv = sb1("mv", [P, NT, 2])
            var = sb1("var", [P, NT])
            lnv = sb1("lnv", [P, NT])
            rs = sb1("rs", [P, NT])
            nw = sb1("nw", [P, NT])
            rstd = sb1("rstd", [P, NT])
            shift = sb1("shift", [P, NT])
            load_x = [sem1(f"load_x{m}") for m in range(4)]
            load_q, load_k, load_o, load_v = [sem1(f"load_w{c}") for c in "qkov"]
            load_s = sem1("load_s")
            load_g = sem1("load_gain")
            made = sem1("made")
            dve_step = sem1("dve1")
            act_step = sem1("act1")
            pe_step = sem1("pe1")

            dve_at, act_at, pe_at = {}, {}, {}

            DVE_TILES = 11

            block = c1.enter_context(nc.Block())

            for n, name in enumerate(["q0", "q1", "k0", "k1", "xT0", "xT1", "xT2", "xT3", "woT0", "woT1"]):
                pe_at[name] = n + 1
            for n, name in enumerate(["ln_v", "rs", "q0", "q1"] + [f"xn{t}" for t in range(DVE_TILES, NT)] +
                                     ["k0", "k1", "xT0", "xTh0", "xT1", "xT2", "woT0"]):
                act_at[name] = n + 1
            steps = ["zero"]
            for m in range(5):
                steps += [f"st{t}" for t in range(4 * m, min(4 * m + 4, NT))]
                steps += [f"mv{t}" for t in range(max(4 * m - 4, 0), 4 * m)]
            steps += ["var", "sign0", "sign", "gain_abs", "cross_c", "score_c0", "score_c"]
            steps += ["nw1", "nw2", "nw3", "rstd", "shift"]
            steps += [f"xn{t}" for t in range(DVE_TILES)]
            steps += ["q0", "q1", "k0", "k1", "xT3", "xTl0", "woT1"]
            for n, name in enumerate(steps):
                dve_at[name] = n + 1

            @block.sync
            def _(sp):
                x_v = x.rearrange("b (h p) d -> p (b h) d", p=P)
                for m in range(4):
                    sp.dma_start(x_in[:, 4 * m:4 * m + 4, :], x_v[:, 4 * m:4 * m + 4, :]).then_inc(load_x[m], 16)
                sp.dma_start(wq_in[:, :, :], Wq.rearrange("(h p) d -> p h d", p=P)).then_inc(load_q, 16)
                sp.dma_start(wk_in[:, :, :], Wk.rearrange("(h p) d -> p h d", p=P)).then_inc(load_k, 16)
                sp.dma_start(wo_in[:, :], Wo).then_inc(load_o, 16)
                sp.dma_start(wv_in[:, :, :], Wv.rearrange("(h p) d -> p h d", p=P)).then_inc(load_v, 16)
                for loaded in (*load_x, load_q, load_k, load_o, load_v):
                    sp.wait_ge(loaded, 16)
                sp.wait_ge(load_g, 16)
                sp.wait_ge(load_s, 48)

            @block.gpsimd
            def _(pool):
                n = 0

                def done(ins):
                    nonlocal n
                    n += 1
                    ins.then_inc(made, 1)
                    pool.wait_ge(made, n)

                done(pool.memset(ident[:, :], 0.0))
                done(pool.affine_select(out=ident[:, :], in_=ident[:, :], compare_op=ALU.not_equal, fill=1.0, base=0,
                                        pattern=[[-1, P]], channel_multiplier=1))
                done(pool.iota(row_i[:, :], pattern=[[1, HT * T]], base=0, channel_multiplier=0))
                done(pool.iota(col_i[:, :], pattern=[[P, HT]], base=0, channel_multiplier=1))
                done(pool.memset(later[:, :], 0.0))
                done(pool.memset(whole[:, :], 0.0))
                done(pool.memset(later[C:P, 0:C], 1.0))
                done(pool.memset(whole[0:C, :], 1.0))
                done(pool.memset(causal[:, :], 0.0))
                for c in range(2):
                    rows = causal[c * C:(c + 1) * C, :]
                    done(pool.affine_select(out=rows, in_=rows, compare_op=ALU.is_ge, fill=NEG, base=0,
                                            pattern=[[-1, C]], channel_multiplier=1))
                done(pool.tensor_copy(ident_b[:, :], ident[:, :]))
                done(pool.tensor_copy(causal_b[:, :, :], bc(causal[:, :].unsqueeze(1), P, G * HT, C)))
                done(pool.memset(AT[:, :, :, :], 0.0))
                assert n == 14

            @block.scalar
            def _(act):
                act.preload_act_table_set("natural_log_exp_and_others")
                act.dma_start(gain_in[:, :], qk_gain.partition_broadcast(P)).then_inc(load_g, 16)
                act.dma_start(gates_w[:, H:H + E], gate_w).then_inc(load_s, 16)
                act.dma_start(gates_w[:, 0:H], Wg.rearrange("h d -> d h"), allow_slow_non_contiguous=True)\
                   .then_inc(load_s, 16)
                act.dma_start(bg_in[:, :], bg.partition_broadcast(P)).then_inc(load_s, 16)
                n = 0

                def done(name, ins):
                    nonlocal n
                    n += 1
                    assert act_at[name] == n, name
                    ins.then_inc(act_step, 1)

                act.wait_ge(dve_step, dve_at["var"])
                done("ln_v", act.activation(lnv[:, :], var[:, :], ACT.Ln))
                act.wait_ge(act_step, act_at["ln_v"])
                done("rs", act.activation(rs[:, :], lnv[:, :], ACT.Exp, scale=-0.5))

                def weight_hi(w, j):
                    name = f"{'qk'[w]}{j}"
                    act.wait_ge(pe_step, pe_at[name])
                    dst = proj_w[:, w, 0, j * GW:(j + 1) * GW]
                    if w:
                        done(name, act.activation(dst, bank[2 + 2 * w + j][:, :], ACT.Copy))
                    else:
                        act.wait_ge(dve_step, dve_at["sign"])
                        done(name, act.activation(dst, bank[2 + 2 * w + j][:, :], ACT.Copy, scale=sign[:, 0:1]))

                weight_hi(0, 0)
                weight_hi(0, 1)
                act.wait_ge(dve_step, dve_at["shift"])
                for t in range(DVE_TILES, NT):
                    done(f"xn{t}", act.activation(xn[:, t, :], x_in[:, t, :], ACT.Identity, scale=rstd[:, t:t + 1],
                                                  bias=shift[:, t:t + 1]))
                weight_hi(1, 0)
                weight_hi(1, 1)
                for m in range(3):
                    act.wait_ge(pe_step, pe_at[f"xT{m}"])
                    src = bank[(6 + m) % 8]
                    done(f"xT{m}", act.activation(xT[:, m * 512:(m + 1) * 512], src[:, :], ACT.Copy))
                    if m == 0:
                        done("xTh0", act.activation(xT_all[:, 0:2, 0, :], src[:, :].rearrange("p (b t) -> p b t", b=2),
                                                    ACT.Copy))
                act.wait_ge(pe_step, pe_at["woT0"])
                done("woT0", act.activation(wo_T[:, 0:G, :].rearrange("p h d -> p (h d)"), bank[6][:, :], ACT.Copy))

            @block.tensor
            def _(pe):
                n = 0

                def done(name, ins):
                    nonlocal n
                    n += 1
                    assert pe_at[name] == n, name
                    ins.then_inc(pe_step, 1)

                pe.wait_ge(made, 2)
                for w, (name, w_in, loaded) in enumerate((("q", wq_in, load_q), ("k", wk_in, load_k))):
                    pe.wait_ge(loaded, 16)
                    for j in range(2):
                        for h in range(G):
                            mm = pe.transpose(bank[2 + 2 * w + j][:, h * P:(h + 1) * P], w_in[:, G * j + h, :],
                                              ident[:, :])
                        done(f"{name}{j}", mm)
                for m in range(4):
                    pe.wait_ge(dve_step, dve_at[f"xn{min(4 * m + 3, DVE_TILES - 1)}"])
                    if 4 * m + 3 >= DVE_TILES:
                        pe.wait_ge(act_step, act_at[f"xn{4 * m + 3}"])
                    for t in range(4):
                        mm = pe.transpose(bank[(6 + m) % 8][:, t * P:(t + 1) * P], xn[:, 4 * m + t, :], ident[:, :])
                    done(f"xT{m}", mm)
                pe.wait_ge(load_o, 16)
                for j in range(2):
                    pe.wait_ge(act_step, act_at[("xTh0", "xT1")[j]])
                    for h in range(G):
                        mm = pe.transpose(bank[6 + j][:, h * P:(h + 1) * P], wo_in[:, (G * j + h) * P:(G * j + h + 1) * P],
                                          ident[:, :])
                    done(f"woT{j}", mm)
            @block.vector
            def _(dve):
                n = 0

                def done(name, ins):
                    nonlocal n
                    n += 1
                    assert dve_at[name] == n, (name, n)
                    ins.then_inc(dve_step, 1)

                def after(name):
                    dve.wait_ge(dve_step, dve_at[name])

                done("zero", dve.memset(mv[:, :, :], 0.0))
                for m in range(4):
                    dve.wait_ge(load_x[m], 16)
                    for t in range(4 * m, 4 * m + 4):
                        done(f"st{t}", dve.bn_stats(stats[:, t, :], x_in[:, t, :]))
                    if m == 0:
                        continue
                    after(f"st{4 * m - 1}")
                    for t in range(4 * m - 4, 4 * m):
                        done(f"mv{t}", dve.bn_aggr(mv[:, t, :], stats[:, t, :]))
                after(f"st{NT - 1}")
                for t in range(NT - 4, NT):
                    done(f"mv{t}", dve.bn_aggr(mv[:, t, :], stats[:, t, :]))
                after(f"mv{NT - 1}")
                done("var", dve.tensor_scalar(var[:, :], mv[:, :, 1], LN_EPS, None, ALU.add))
                dve.wait_ge(load_g, 16)
                done("sign0", dve.tensor_scalar(sign[:, :], gain_in[:, :], 0.0, 2.0, ALU.is_ge, ALU.mult))
                after("sign0")
                done("sign", dve.tensor_scalar(sign[:, :], sign[:, :], -1.0, None, ALU.add))
                after("sign")
                done("gain_abs", dve.tensor_tensor(gain_abs[:, :], gain_in[:, :], sign[:, :], ALU.mult))
                after("gain_abs")
                done("cross_c", dve.tensor_scalar(cross_c[:, :], gain_abs[:, :], 1.0 / (UNIT * UNIT), None, ALU.mult))
                done("score_c0", dve.tensor_scalar(score_c[:, :], gain_abs[:, :], TINY, None, ALU.max))
                after("score_c0")
                done("score_c", dve.tensor_scalar(score_c[:, :], score_c[:, :], 1.0 / (math.sqrt(P) * UNIT * UNIT), None,
                                                  ALU.mult))
                dve.wait_ge(act_step, act_at["rs"])
                done("nw1", dve.tensor_tensor(nw[:, :], rs[:, :], rs[:, :], ALU.mult))
                after("nw1")
                done("nw2", dve.tensor_tensor(nw[:, :], nw[:, :], var[:, :], ALU.mult))
                after("nw2")
                done("nw3", dve.tensor_scalar(nw[:, :], nw[:, :], -0.5, 1.5, ALU.mult, ALU.add))
                after("nw3")
                done("rstd", dve.tensor_tensor(rstd[:, :], rs[:, :], nw[:, :], ALU.mult))
                after("rstd")
                done("shift", dve.scalar_tensor_tensor(out=shift[:, :], in0=mv[:, :, 0], scalar=-1.0, in1=rstd[:, :],
                                                       op0=ALU.mult, op1=ALU.mult))
                for t in range(DVE_TILES):
                    done(f"xn{t}", dve.tensor_scalar(xn[:, t, :], x_in[:, t, :], mv[:, t, 0:1], rstd[:, t:t + 1],
                                                     ALU.subtract, ALU.mult))
                for w, name in enumerate("qk"):
                    for j in range(2):
                        dve.wait_ge(act_step, act_at[f"{name}{j}"])
                        cols = slice(j * GW, (j + 1) * GW)
                        src, hi, lo = bank[2 + 2 * w + j], proj_w[:, w, 0, cols].bitcast(fp32), proj_w[:, w, 1, cols]
                        if w:
                            done(f"{name}{j}", dve.tensor_tensor(lo, src[:, :], hi, ALU.subtract))
                        else:
                            done(f"{name}{j}", dve.scalar_tensor_tensor(out=lo, in0=src[:, :], scalar=sign[:, 0:1],
                                                                        in1=hi, op0=ALU.mult, op1=ALU.subtract))
                dve.wait_ge(pe_step, pe_at["xT3"])
                done("xT3", dve.tensor_copy(xT[:, 3 * 512:], bank[1][:, :]))
                dve.wait_ge(act_step, act_at["xTh0"])
                done("xTl0", dve.tensor_tensor(xT_all[:, 0:2, 1, :], xT[:, 0:512].rearrange("p (b t) -> p b t", b=2),
                                               xT_all[:, 0:2, 0, :].bitcast(fp32), ALU.subtract))
                dve.wait_ge(pe_step, pe_at["woT1"])
                done("woT1", dve.tensor_copy(wo_T[:, G:2 * G, :].rearrange("p h d -> p (h d)"), bank[7][:, :]))
                assert n == len(steps)

        NB = 4
        FIND = 8
        with ExitStack() as c2:
            def sb2(name, shape, dt=fp32):
                return c2.enter_context(nc.sbuf_tensor(name, shape, dt))

            def sem2(name):
                return c2.enter_context(nc.semaphore(name))

            def sems2(name, n):
                return [sem2(f"{name}{i}") for i in range(n)]

            onehot = [sb2(f"onehot{i}", [P, HT, E * K], fp16) for i in range(2)]
            tok_bc = [sb2(f"tok_bc{i}", [P, E * K], fp16) for i in range(2)]
            xs = sb2("xs", [P, 2, T], fp32r)
            z = sb2("z", [P, NT, H])
            za = sb2("za", [P, NT, H])
            zn = sb2("zn", [P, NT, H])
            logg = sb2("logg", [P, NT, H])
            gmax = sb2("gmax", [P, NT])
            gsh = sb2("gsh", [P, NT, E])
            gsum = sb2("gsum", [P, NT])
            ginv = sb2("ginv", [P, NT])
            probs = sb2("probs", [P, HT, B, E])
            top = sb2("top", [B * E, 2, K])
            top_i = sb2("top_i", [B * E, K], u32)
            best = sb2("best", [B * E, TOPS])
            best_i = sb2("best_i", [B * E, TOPS], u32)
            held = sb2("held", [B * E, 2])
            left_next = sb2("left_next", [B * E, T])
            top_t = sb2("top_t", [B * E, 2, K])
            qk = [sb2(f"qk{i}", [P, NB, GW]) for i in range(2)]
            junk = sb2("junk", [P, NB, G, P], bf16)
            ssq = [sb2(f"ssq{i}", [P, NB * G]) for i in range(2)]
            ms = sb2("ms", [P, NB * G])
            eps_c = sb2("eps_c", [P, NB * G])
            three_c = sb2("three_c", [P, NB * G])
            lms = sb2("lms", [P, NB * G])
            r0 = sb2("r0", [P, NB * G])
            nt = sb2("nt", [P, NB * G])
            vS = [sb2(f"vS{i}", [P, HT, GW]) for i in range(2)]
            qT = [sb2(f"qT{i}", [P, 2, G, T], fp16) for i in range(2)]
            kT = [sb2(f"kT{i}", [P, 2, G, T], fp16) for i in range(2)]
            sc = sb2("sc", [P, G * HT, C])
            ex = sb2("ex", [P, G * HT, C])
            smax = sb2("smax", [P, G * HT])
            ssum = sb2("ssum", [P, G * HT])
            sinv = sb2("sinv", [P, G * HT])

            s_zero = sem2("s_zero")
            split_s = sem2("tokens_split")
            xs_loaded = sem2("xs_loaded")
            experts_s = sem2("experts_loaded")
            pj = sems2("projected", 6)
            sq = sems2("squared", NB)
            raw = sems2("raw_copied", NB)
            vcp = sems2("v_copied", 2)
            mean = sems2("mean_sq", 2)
            lnm = sems2("ln_mean", 2)
            rsq = sems2("rsqrt", 2)
            newt = sem2("newton")
            nrm = sems2("normalised", 2)
            tr = sems2("transposed", NB)
            hi_s = sems2("hi_copied", NB)
            lo_s = sems2("lo_copied", NB)
            cross_s = sems2("cross_scores", 2)
            diag_s = sem2("chunk_scores")
            maxed = sem2("maxed")
            shifted = sem2("shifted")
            exped = sem2("exped")
            summed = sem2("summed")
            inverted = sem2("inverted")
            attn_s = sem2("attn_ready")
            ta = sem2("attn_turned")
            at_s = sem2("attn_T_copied")
            crossed = sems2("cross_weights", 2)
            av = sem2("weighted_values")
            summed_out = sem2("residual_added")
            topk = sem2("topk")
            rows_s = sem2("token_rows")
            early_pe = sem2("early_pe")
            early_act = sem2("early_act")
            masks_s = sem2("masks_made")
            early_dve = sem2("early_dve")
            pe_n = {name: n + 1 for n, name in enumerate(["logits", "n0", "n1", "decay", "probsT"])}
            act_n = {name: n + 1 for n, name in enumerate(["zexp", "zln", "gexp", "n0", "n1", "decay2", "decay3"])}
            dve_n = {name: n + 1 for n, name in enumerate(["z", "zn", "za", "gmax", "gsh", "logg", "gsum", "ginv",
                                                           "probs", "n0", "n1", "decay", "left"])}
            slots = sem2("slots_turned")
            asked = sem2("tokens_spread")
            spread = sem2("tokens_copied")
            hot = sem2("onehots")
            gath = sem2("gathered")
            gath_h = sem2("gathered_hi")
            gath_l = sem2("gathered_lo")

            PJB = [bank[0], bank[1], bank[6]]
            TRB = [bank[2], bank[3]]
            DB, XB, OB = bank[4], bank[5], bank[7]

            block = c2.enter_context(nc.Block())

            @block.sync
            def _(sp):
                src = xT_all[:, :, :, :].bitcast(fp32).rearrange("p b c t -> p b (c t)")
                dst = xs[:, :, :].bitcast(fp32).rearrange("p c t -> p (c t)")
                sp.wait_ge(split_s, 2)
                sp.dma_start(dst, src[:, 2, :]).then_inc(xs_loaded, 16)
                sp.wait_ge(early_pe, pe_n["n1"])
                sp.wait_ge(split_s, 6)
                sp.dma_start(w1_in[:, :, :], w1.rearrange("e d f -> d e f")).then_inc(experts_s, 16)
                sp.dma_start(w2_in[:, :, :], w2.rearrange("e (f p) d -> p (e f) d", p=P)).then_inc(experts_s, 16)
                with sp.Fori(3, B) as b:
                    sp.wait_ge(pj[5], 2 * b)
                    sp.dma_start(dst, src[:, ds(b, 1), :].rearrange("p o t -> p (o t)")).then_inc(xs_loaded, 16)
                sp.wait_ge(xs_loaded, 16 * (B - 2))
                sp.wait_ge(experts_s, 32)

            @block.tensor
            def _(pe):
                def project(b, g, k, fresh=False):
                    u = 2 * b + g
                    if isinstance(b, int) and b < 2:
                        x_T = xT_all[:, b, :, :]
                    else:
                        pe.wait_ge(xs_loaded, 16 * (b - 1))
                        x_T = xs[:, :, :]
                    tile, w = (k // 2, k % 2) if k < NB else (k - NB, 2)
                    if k >= 3:
                        pe.wait_ge(raw[k - 3], u + 1)
                    elif not fresh:
                        pe.wait_ge((raw[3], vcp[0], vcp[1])[k], u)
                    for n, (a_, b_) in enumerate(((1, 0), (0, 1), (0, 0))):
                        mm = pe.matmul(PJB[k % 3][:, :], x_T[:, a_, tile * P:(tile + 1) * P],
                                       proj_w[:, w, b_, g * GW:(g + 1) * GW], start=(n == 0), stop=(n == 2))
                    mm.then_inc(pj[k], 1)

                def turn(b, g, k, fresh=False):
                    u = 2 * b + g
                    pe.wait_ge(nrm[k // 2], u + 1)
                    if k >= 2:
                        pe.wait_ge(lo_s[k - 2], u + 1)
                    elif not fresh:
                        pe.wait_ge(lo_s[k + 2], u)
                    for h in range(G):
                        mm = pe.transpose(TRB[k % 2][:, h * P:(h + 1) * P], qk[g][:, k, h * P:(h + 1) * P], ident[:, :])
                    mm.then_inc(tr[k], 1)

                PARTS = ((1, 0), (0, 1), (0, 0))

                def cross(b, g, n, fresh=False):
                    u = 2 * b + g
                    if n == 0:
                        pe.wait_ge(lo_s[NB - 1], u + 1)
                        if fresh:
                            pe.wait_ge(early_dve, dve_n["left"])
                        else:
                            pe.wait_ge(crossed[1], u)
                    else:
                        pe.wait_ge(crossed[0], u + 1)
                    for hh in range(2):
                        h, o = 2 * n + hh, hh * T
                        for m, (a_, b_) in enumerate(PARTS):
                            pe.matmul(XB[:, o:o + 3 * C], kT[g][:, a_, h, 0:P], qT[g][:, b_, h, C:T],
                                      start=(m == 0), stop=(m == 2))
                        for m, (a_, b_) in enumerate(PARTS):
                            mm = pe.matmul(XB[0:C, o + 3 * C:o + T], kT[g][:, a_, h, P:P + C], qT[g][:, b_, h, 3 * C:T],
                                           start=(m == 0), stop=(m == 2))
                    mm.then_inc(cross_s[n], 1)

                def chunk(b, g, fresh=False):
                    if not fresh:
                        pe.wait_ge(at_s, 2 * b + g)
                    else:
                        pe.wait_ge(early_act, act_n["decay3"])
                    pe.matmul(DB[:, :], ident_b[:, :], causal_b[:, :, :].rearrange("p j s -> p (j s)"), start=True,
                              stop=False, skip_group_check=True)
                    for h in range(G):
                        for t in range(HT):
                            for c in range(2):
                                o = t * P + c * C
                                for m, (a_, b_) in enumerate(PARTS):
                                    mm = pe.matmul(DB[c * C:(c + 1) * C, (h * HT + t) * C:(h * HT + t + 1) * C],
                                                   qT[g][:, a_, h, o:o + C], kT[g][:, b_, h, o:o + C],
                                                   start=False, stop=(m == 2), skip_group_check=True)
                    mm.then_inc(diag_s, 1)

                def turn_attn(b, g):
                    pe.wait_ge(attn_s, 2 * b + g + 1)
                    for h in range(G):
                        mm = pe.transpose(DB[:, h * P:(h + 1) * P], ex[:, h * HT:(h + 1) * HT, :].rearrange("p t s -> p (t s)"),
                                          ident[:, :])
                    mm.then_inc(ta, 1)

                def values(b, g, h, fresh=False):
                    u = 2 * b + g
                    if h == 0:
                        pe.wait_ge(at_s, u + 1)
                        pe.wait_ge(crossed[1], u + 1)
                        pe.wait_ge(vcp[1], u + 1)
                        if g == 0 and not fresh:
                            pe.wait_ge(summed_out, b)
                    for n, (blk, src, dst) in enumerate(((0, 0, 0), (2, 0, 1), (1, 1, 1))):
                        mm = pe.matmul(OB[:, dst * D:(dst + 1) * D], AT[:, h, blk, :],
                                       vS[g][:, src, h * P:(h + 1) * P], start=(g == 0 and h == 0 and n == 0),
                                       stop=(g == 1 and h == G - 1 and n > 0), skip_group_check=True)
                    if h == G - 1:
                        mm.then_inc(av, 1)

                def ask(j, k, first=False):
                    if first:
                        pe.wait_ge(raw[3] if k == 0 else vcp[0], 2 * B)
                    else:
                        pe.wait_ge(spread, 2 * j + k - 1)
                    pe.matmul(bank[k][:, :], pick_b[:, ds(2 * j + k, 1), :].rearrange("p o t -> p (o t)"),
                              tok_spread[:, :], start=True, stop=True).then_inc(asked, 1)

                def gather(j, k, first=False):
                    b = 2 * j + k
                    pe.wait_ge(hot, b + 1)
                    if first:
                        pe.wait_ge(lo_s[2 + k], 2 * B)
                    else:
                        pe.wait_ge(gath_l, b - 1)
                    for n, (rows, t) in enumerate(((xn_l, 0), (xn_l, 1), (xn_h, 0), (xn_h, 1))):
                        mm = pe.matmul(bank[2 + k][:, :], rows[:, ds(HT * b + t, 1), :].rearrange("p o d -> p (o d)"),
                                       onehot[k][:, t, :], start=(n == 0), stop=(n == 3))
                    mm.then_inc(gath, 1)

                def step(b, g, fresh=False, before_last=False):
                    nb, ng = (b, 1) if g == 0 else (b + 1, 0)
                    pb, pg = (b, 0) if g == 1 else (b - 1, 1)
                    project(nb, ng, 0)
                    turn(b, g, 1)
                    project(nb, ng, 1)
                    project(nb, ng, 2)
                    turn(b, g, 2)
                    turn_attn(pb, pg)
                    turn(b, g, 3)
                    project(nb, ng, 3)
                    if not before_last:
                        project(nb, ng, 4)
                    for h in range(G):
                        values(pb, pg, h, fresh)
                    if not before_last:
                        project(nb, ng, 5)
                    cross(b, g, 0)
                    chunk(b, g)
                    turn(nb, ng, 0)
                    cross(b, g, 1)

                def turn_slots():
                    pe.wait_ge(topk, FIND * (K // TOPS) + 2)
                    pe.wait_ge(vcp[1], 2 * B)
                    pe.transpose(bank[6][:, 0:B * E], top[:, :, :].rearrange("p a k -> p (a k)"),
                                 ident[0:B * E, 0:B * E])
                    pe.transpose(bank[6][:, 64:64 + B * E], top_t[:, :, :].rearrange("p a k -> p (a k)"),
                                 ident[0:B * E, 0:B * E]).then_inc(slots, 1)

                def last_step(b, g):
                    turn(b, g, 1)
                    pe.wait_ge(topk, FIND * (K // TOPS) + 3)
                    ask(0, 0, first=True)
                    project(b, g, 4)
                    turn(b, g, 2)
                    project(b, g, 5)
                    turn_attn(b, 0)
                    ask(0, 1, first=True)
                    turn(b, g, 3)
                    turn_slots()
                    values(b, 0, 0)
                    values(b, 0, 1)
                    pe.wait_ge(rows_s, 2 * B)
                    for k in range(2):
                        ask(1, k)
                        gather(0, k, first=True)
                    cross(b, g, 0)
                    chunk(b, g)
                    values(b, 0, 2)
                    values(b, 0, 3)
                    cross(b, g, 1)
                    for k in range(2):
                        gather(1, k)
                        ask(2, k)
                    turn_attn(b, g)
                    for k in range(2):
                        gather(2, k)
                        ask(3, k)
                    for h in range(2):
                        values(b, g, h)
                    for k in range(2):
                        gather(3, k)
                    for h in range(2, G):
                        values(b, g, h)

                def router_logits():
                    for t in range(NT):
                        mm = pe.matmul(DB[:, t * (H + E):(t + 1) * (H + E)], xT[:, t * P:(t + 1) * P], gates_w[:, :],
                                       start=True, stop=True)
                    mm.then_inc(early_pe, 1)

                def value_weights():
                    for j in range(2):
                        for h in range(G):
                            mm = pe.matmul((XB, OB)[j][:, h * P:(h + 1) * P], wv_in[:, G * j + h, :],
                                           wo_T[:, G * j + h, :], start=True, stop=True)
                        mm.then_inc(early_pe, 1)

                def log_decays():
                    pe.wait_ge(early_dve, dve_n["logg"])
                    by_tile = logg[:, :, :].rearrange("p (b t) h -> p t b h", t=HT)
                    BH = B * H
                    pe.matmul(DB[:, 0:BH], later[:, :], by_tile[:, 0], start=True, stop=True)
                    pe.matmul(DB[:, BH:2 * BH], later[:, :], by_tile[:, 0], start=True, stop=False)
                    pe.matmul(DB[:, BH:2 * BH], whole[:, :], by_tile[:, 1], start=False, stop=True)\
                      .then_inc(early_pe, 1)

                def turn_probs():
                    pe.wait_ge(early_dve, dve_n["probs"])
                    for t in range(HT):
                        mm = pe.transpose(XB[0:B * E, t * P:(t + 1) * P],
                                          probs[:, t, :, :].rearrange("p b e -> p (b e)"), ident[:, :])
                    mm.then_inc(early_pe, 1)

                for k in range(4):
                    project(0, 0, k, fresh=True)
                router_logits()
                turn(0, 0, 0, fresh=True)
                project(0, 1, 0)
                turn(0, 0, 1, fresh=True)
                pe.wait_ge(raw[1], 1)
                project(0, 1, 1, fresh=True)
                pe.wait_ge(raw[2], 1)
                project(0, 1, 2, fresh=True)
                turn(0, 0, 2)
                turn(0, 0, 3)
                value_weights()
                log_decays()
                project(0, 1, 3)
                pe.wait_ge(early_dve, dve_n["n1"])
                pe.wait_ge(raw[1], 2)
                project(0, 0, 4)
                pe.wait_ge(raw[2], 2)
                project(0, 0, 5)
                turn_probs()
                pe.wait_ge(vcp[0], 1)
                project(0, 1, 4)
                pe.wait_ge(vcp[1], 1)
                project(0, 1, 5)
                cross(0, 0, 0, fresh=True)
                chunk(0, 0, fresh=True)
                turn(0, 1, 0)
                cross(0, 0, 1)
                step(0, 1, fresh=True)
                step(1, 0)
                with pe.Fori(1, B - 2) as j:
                    step(j, 1)
                    step(j + 1, 0)
                step(B - 2, 1)
                step(B - 1, 0, before_last=True)
                last_step(B - 1, 1)

            @block.scalar
            def _(act):
                def square(b, g, k, fresh=False):
                    u = 2 * b + g
                    act.wait_ge(pj[k], u + 1)
                    if not fresh:
                        act.wait_ge(sq[k], u)
                        act.wait_ge(nrm[k // 2], u - 1)
                    for h in range(G):
                        ins = act.activation(junk[:, k, h, :], PJB[k % 3][:, h * P:(h + 1) * P], ACT.Square,
                                             accum_out=ssq[g][:, k * G + h:k * G + h + 1])
                    ins.then_inc(sq[k], 1)

                def rsqrt(b, g, t):
                    u = 2 * b + g
                    cols = slice(t * 2 * G, (t + 1) * 2 * G)
                    act.wait_ge(mean[t], u + 1)
                    act.activation(lms[:, cols], ms[:, cols], ACT.Ln, scale=1.0 / P).then_inc(lnm[t], 1)
                    act.wait_ge(lnm[t], u + 1)
                    act.activation(r0[:, cols], lms[:, cols], ACT.Exp, scale=-0.5).then_inc(rsq[t], 1)

                def hi(b, g, k):
                    dst = (qT, kT)[k % 2][g][:, 0, :, (k // 2) * P:(k // 2 + 1) * P]
                    act.wait_ge(tr[k], 2 * b + g + 1)
                    act.activation(dst, TRB[k % 2][:, :].rearrange("p (h t) -> p h t", h=G), ACT.Copy)\
                       .then_inc(hi_s[k], 1)

                def value(b, g, t, fresh=False):
                    u = 2 * b + g
                    act.wait_ge(pj[NB + t], u + 1)
                    if not fresh:
                        act.wait_ge(av, u - 1)
                    act.activation(vS[g][:, t, :], PJB[1 + t][:, :], ACT.Copy).then_inc(vcp[t], 1)

                def exps(b, g):
                    act.wait_ge(shifted, 2 * b + g + 1)
                    act.activation(ex[:, :, :], sc[:, :, :], ACT.Exp, scale=score_c[:, 0:1]).then_inc(exped, 1)

                def attn_T(b, g):
                    act.wait_ge(ta, 2 * b + g + 1)
                    for t in range(HT):
                        for c in range(2):
                            rows = slice(c * C, (c + 1) * C)
                            ins = act.activation(AT[rows, :, t, rows],
                                                 DB[t * C:(t + 1) * C, :].rearrange("p (h c) -> p h c", h=G)[:, :, rows],
                                                 ACT.Copy)
                    ins.then_inc(at_s, 1)

                def copy_tokens(j, k, first=False):
                    act.wait_ge(asked, 2 * j + k + 1)
                    if not first:
                        act.wait_ge(hot, 2 * j + k - 1)
                    act.activation(tok_bc[k][:, :], bank[k][:, :], ACT.Copy).then_inc(spread, 1)

                def gathered_hi(j, k):
                    b = 2 * j + k
                    act.wait_ge(gath, b + 1)
                    act.activation(picked[0][:, :, ds(K * b, K)], bank[2 + k][:, :].rearrange("p (e s) -> p e s", e=E),
                                   ACT.Copy).then_inc(gath_h, 1)

                def step(b, g, fresh=False, before_last=False):
                    nb, ng = (b, 1) if g == 0 else (b + 1, 0)
                    pb, pg = (b, 0) if g == 1 else (b - 1, 1)
                    hi(b, g, 0)
                    exps(pb, pg)
                    square(nb, ng, 0)
                    hi(b, g, 1)
                    square(nb, ng, 1)
                    attn_T(pb, pg)
                    rsqrt(nb, ng, 0)
                    hi(b, g, 2)
                    hi(b, g, 3)
                    square(nb, ng, 2)
                    square(nb, ng, 3)
                    if not before_last:
                        value(nb, ng, 0, fresh)
                    rsqrt(nb, ng, 1)
                    if not before_last:
                        value(nb, ng, 1, fresh)

                def last_step(b, g):
                    hi(b, g, 0)
                    exps(b, 0)
                    hi(b, g, 1)
                    copy_tokens(0, 0, first=True)
                    value(b, g, 0)
                    hi(b, g, 2)
                    value(b, g, 1)
                    attn_T(b, 0)
                    copy_tokens(0, 1, first=True)
                    hi(b, g, 3)
                    for k in range(2):
                        copy_tokens(1, k)
                        gathered_hi(0, k)
                    exps(b, g)
                    for k in range(2):
                        gathered_hi(1, k)
                        copy_tokens(2, k)
                    attn_T(b, g)
                    for k in range(2):
                        gathered_hi(2, k)
                        copy_tokens(3, k)
                    act.preload_act_table_set("gelu_apprx_tanh_and_others")
                    for k in range(2):
                        gathered_hi(3, k)

                def router_exps():
                    act.wait_ge(early_dve, dve_n["za"])
                    act.activation(za[:, :, :], za[:, :, :], ACT.Exp, scale=-1.0).then_inc(early_act, 1)
                    act.wait_ge(early_act, act_n["zexp"])
                    act.activation(za[:, :, :], za[:, :, :], ACT.Ln, bias=1.0).then_inc(early_act, 1)
                    act.wait_ge(early_dve, dve_n["gsh"])
                    act.activation(gsh[:, :, :], gsh[:, :, :], ACT.Exp).then_inc(early_act, 1)

                def value_weights_hi():
                    for j in range(2):
                        act.wait_ge(early_pe, pe_n[f"n{j}"])
                        act.activation(proj_w[:, 2, 0, j * GW:(j + 1) * GW], (XB, OB)[j][:, :], ACT.Copy)\
                           .then_inc(early_act, 1)

                def decays():
                    act.wait_ge(early_pe, pe_n["decay"])
                    for k in range(2):
                        act.activation(decay[:, :, :, k].rearrange("p b h -> p (b h)"),
                                       DB[:, k * B * H:(k + 1) * B * H], ACT.Exp, scale=-1.0).then_inc(early_act, 1)

                square(0, 0, 0, fresh=True)
                square(0, 0, 1, fresh=True)
                rsqrt(0, 0, 0)
                square(0, 0, 2, fresh=True)
                square(0, 0, 3, fresh=True)
                rsqrt(0, 0, 1)
                router_exps()
                hi(0, 0, 0)
                square(0, 1, 0, fresh=True)
                hi(0, 0, 1)
                square(0, 1, 1, fresh=True)
                rsqrt(0, 1, 0)
                hi(0, 0, 2)
                hi(0, 0, 3)
                value_weights_hi()
                decays()
                square(0, 1, 2, fresh=True)
                square(0, 1, 3, fresh=True)
                value(0, 0, 0, fresh=True)
                value(0, 0, 1, fresh=True)
                rsqrt(0, 1, 1)
                value(0, 1, 0, fresh=True)
                value(0, 1, 1, fresh=True)
                step(0, 1)
                step(1, 0)
                with act.Fori(1, B - 2) as j:
                    step(j, 1)
                    step(j + 1, 0)
                step(B - 2, 1)
                step(B - 1, 0, before_last=True)
                last_step(B - 1, 1)

            @block.gpsimd
            def _(pool):
                pool.memset(eps_c[:, :], P * RMS_EPS).then_inc(s_zero, 1)
                pool.memset(three_c[:, :], 3.0 * P).then_inc(s_zero, 1)
                pool.wait_ge(s_zero, 2)

                def split_tokens(m):
                    src = xT[:, m * 512:(m + 1) * 512].rearrange("p (b t) -> p b t", b=2)
                    hi, lo = xT_all[:, 2 * m:2 * m + 2, 0, :], xT_all[:, 2 * m:2 * m + 2, 1, :]
                    pool.tensor_copy(hi, src).then_inc(split_s, 1)
                    pool.wait_ge(split_s, 2 * m - 1)
                    pool.tensor_tensor(lo, src, hi.bitcast(fp32), ALU.subtract).then_inc(split_s, 1)

                def normalise(b, g, t):
                    u = 2 * b + g
                    cols = slice(t * 2 * G, (t + 1) * 2 * G)
                    pool.wait_ge(sq[2 * t + 1], u + 1)
                    pool.tensor_tensor(ms[:, cols], ssq[g][:, cols], eps_c[:, cols], ALU.add).then_inc(mean[t], 1)
                    n0 = 8 * u + 4 * t
                    pool.wait_ge(rsq[t], u + 1)
                    pool.tensor_tensor(nt[:, cols], r0[:, cols], r0[:, cols], ALU.mult).then_inc(newt, 1)
                    pool.wait_ge(newt, n0 + 1)
                    pool.tensor_tensor(nt[:, cols], nt[:, cols], ms[:, cols], ALU.mult).then_inc(newt, 1)
                    pool.wait_ge(newt, n0 + 2)
                    pool.tensor_tensor(nt[:, cols], three_c[:, cols], nt[:, cols], ALU.subtract).then_inc(newt, 1)
                    pool.wait_ge(newt, n0 + 3)
                    pool.tensor_tensor(nt[:, cols], nt[:, cols], r0[:, cols], ALU.mult).then_inc(newt, 1)
                    pool.wait_ge(newt, n0 + 4)
                    pool.wait_ge(raw[2 * t + 1], u + 1)
                    rows = qk[g][:, 2 * t:2 * t + 2, :].rearrange("p k (h d) -> p (k h) d", h=G)
                    pool.tensor_tensor(rows, rows, bc(nt[:, cols].unsqueeze(2), P, 2 * G, P), ALU.mult)\
                        .then_inc(nrm[t], 1)

                def token_rows(b):
                    rows = ds(HT * b, HT)
                    pool.tensor_copy(xn_h[:, rows, :], xn[:, rows, :]).then_inc(rows_s, 1)
                    pool.wait_ge(rows_s, 2 * b + 1)
                    pool.tensor_tensor(xn_l[:, rows, :], xn[:, rows, :], xn_h[:, rows, :], ALU.subtract)\
                        .then_inc(rows_s, 1)

                def normalise_unit(b, g):
                    for t in range(HT):
                        normalise(b, g, t)

                normalise_unit(0, 0)
                normalise_unit(0, 1)
                split_tokens(1)
                normalise_unit(1, 0)
                split_tokens(2)
                normalise_unit(1, 1)
                split_tokens(3)
                normalise_unit(2, 0)
                token_rows(0)
                normalise_unit(2, 1)
                token_rows(1)
                with pool.Fori(3, B) as b:
                    normalise_unit(b, 0)
                    token_rows(b - 1)
                    normalise_unit(b, 1)
                token_rows(B - 1)
                pool.wait_ge(experts_s, 32)
                for e in range(2):
                    pool.tensor_copy(w1_hl[e][:, 0, :], w1_in[:, e, :]).then_inc(w1h_s[e], 1)
                    pool.wait_ge(w1h_s[e], 1)
                    pool.tensor_tensor(w1_hl[e][:, 1, :], w1_in[:, e, :], w1_hl[e][:, 0, :].bitcast(fp32),
                                       ALU.subtract).then_inc(w1l_s[e], 1)

            @block.vector
            def _(dve):
                def raw_copy(b, g, k):
                    dve.wait_ge(sq[k], 2 * b + g + 1)
                    dve.tensor_copy(qk[g][:, k, :], PJB[k % 3][:, :]).then_inc(raw[k], 1)

                def lo(b, g, k):
                    cols = slice((k // 2) * P, (k // 2 + 1) * P)
                    w = (qT, kT)[k % 2][g]
                    dve.wait_ge(hi_s[k], 2 * b + g + 1)
                    dve.tensor_tensor(w[:, 1, :, cols], TRB[k % 2][:, :].rearrange("p (h t) -> p h t", h=G),
                                      w[:, 0, :, cols], ALU.subtract).then_inc(lo_s[k], 1)

                def softmax_shift(b, g):
                    u = 2 * b + g
                    dve.wait_ge(diag_s, u + 1)
                    scores = DB[:, :].rearrange("p (j s) -> p j s", s=C)
                    dve.tensor_reduce(smax[:, :], scores, AX.X, ALU.max).then_inc(maxed, 1)
                    dve.wait_ge(maxed, u + 1)
                    dve.tensor_tensor(sc[:, :, :], scores, bc(smax[:, :].unsqueeze(2), P, G * HT, C),
                                      ALU.subtract).then_inc(shifted, 1)

                def softmax_norm(b, g):
                    u = 2 * b + g
                    dve.wait_ge(exped, u + 1)
                    dve.reduce_sum(ssum[:, :], ex[:, :, :], AX.X).then_inc(summed, 1)
                    dve.wait_ge(summed, u + 1)
                    dve.reciprocal(sinv[:, :], ssum[:, :]).then_inc(inverted, 1)
                    dve.wait_ge(inverted, u + 1)
                    dve.tensor_tensor(ex[:, :, :], ex[:, :, :], bc(sinv[:, :].unsqueeze(2), P, G * HT, C), ALU.mult)\
                       .then_inc(attn_s, 1)

                def cross_weights(b, g, n):
                    dve.wait_ge(cross_s[n], 2 * b + g + 1)
                    src = XB[:, :].rearrange("p (h t) -> p h t", h=2)
                    heads = slice(2 * n, 2 * n + 2)
                    ends = XB[0:C, :].rearrange("p (h k t) -> p h k t", h=2, t=C)[:, :, 0:4:3, :]
                    dve.tensor_scalar(AT[0:C, heads, 0:2, C:P], ends, cross_c[0:C, 0:1], None, ALU.mult)
                    w = decay[:, ds(b, 1), g * G + 2 * n:g * G + 2 * n + 2, :].rearrange("p o h k -> p (o h) k")
                    dve.tensor_tensor(AT[:, heads, 2, :].rearrange("p h (k t) -> p h k t", k=2),
                                      src[:, :, C:3 * C].rearrange("p h (k t) -> p h k t", k=2),
                                      bc(w.unsqueeze(3), P, 2, 2, C), ALU.mult).then_inc(crossed[n], 1)

                def residual(b):
                    dve.wait_ge(av, 2 * b + 2)
                    rows = x_in[:, ds(HT * b, HT), :].rearrange("p h d -> p (h d)")
                    dve.tensor_tensor(rows, rows, OB[:, 0:T], ALU.add).then_inc(summed_out, 1)

                def find(r):
                    if not isinstance(r, int) or r:
                        dve.wait_ge(topk, FIND * r - 3)
                        dve.tensor_copy(top[:, 0, ds((r - 1) * TOPS, TOPS)], best[:, :]).then_inc(topk, 1)
                        dve.tensor_copy(top_i[:, ds((r - 1) * TOPS, TOPS)], best_i[:, :]).then_inc(topk, 1)
                        dve.tensor_copy(left[:, :], left_next[:, :]).then_inc(topk, 1)
                        dve.wait_ge(topk, FIND * r)
                    dve.tensor_copy(held[:, 0:1], left[:, 0:1]).then_inc(topk, 1)
                    dve.max(best[:, :], left[:, :]).then_inc(topk, 1)
                    dve.wait_ge(topk, FIND * r + 2)
                    dve.tensor_copy(held[:, 1:2], best[:, 0:1]).then_inc(topk, 1)
                    dve.max_index(best_i[:, :], best[:, :], left[:, :]).then_inc(topk, 1)
                    dve.match_replace(left_next[:, :], best[:, :], left[:, :], -1.0).then_inc(topk, 1)

                def onehots(j, k, first=False):
                    b = 2 * j + k
                    dve.wait_ge(spread, b + 1)
                    if not first:
                        dve.wait_ge(gath, b - 1)
                    for t in range(HT):
                        ins = dve.tensor_scalar(onehot[k][:, t, :], tok_bc[k][:, :], tok_col[:, t:t + 1], None,
                                                ALU.is_equal)
                    ins.then_inc(hot, 1)

                def gathered_lo(j, k):
                    b = 2 * j + k
                    dve.wait_ge(gath_h, b + 1)
                    dve.tensor_tensor(picked[1][:, :, ds(K * b, K)],
                                      bank[2 + k][:, :].rearrange("p (e s) -> p e s", e=E),
                                      picked[0][:, :, ds(K * b, K)].bitcast(fp32), ALU.subtract).then_inc(gath_l, 1)

                def tokens_of_slots():
                    done = FIND * (K // TOPS)
                    dve.wait_ge(topk, done - 3)
                    dve.tensor_copy(top[:, 0, (K // TOPS - 1) * TOPS:], best[:, :]).then_inc(topk, 1)
                    dve.tensor_copy(top_i[:, (K // TOPS - 1) * TOPS:], best_i[:, :]).then_inc(topk, 1)
                    dve.wait_ge(topk, done - 1)
                    dve.tensor_copy(top[:, 1, :], top[:, 0, :]).then_inc(topk, 1)
                    dve.tensor_copy(top_t[:, 0, :], top_i[:, :]).then_inc(topk, 1)
                    dve.tensor_copy(top_t[:, 1, :], top_i[:, :]).then_inc(topk, 1)
                    dve.wait_ge(topk, done + 2)
                    dve.tensor_tensor(
                        tok_spread[:, :].rearrange("p (e k) -> p e k", e=E), bc(top_t[:, 0, :].unsqueeze(1), B * E, E, K),
                        bc(emask[:, :].unsqueeze(2), B * E, E, K), ALU.mult).then_inc(topk, 1)

                def slot_rows():
                    dve.wait_ge(slots, 1)
                    for dst, at in ((slot_gate, 0), (slot_tok, 64)):
                        for odd in range(2):
                            rows = slice(odd * K, (odd + 1) * K)
                            src = bank[6][rows, at:at + B * E].rearrange("p (bp o e) -> p o e bp", o=2, e=E)[:, odd]
                            dve.tensor_scalar(dst[rows, :, :], src, float(T * odd * (at > 0)), None, ALU.add)

                def step(b, g, turn=None, before_last=False):
                    nb, ng = (b, 1) if g == 0 else (b + 1, 0)
                    pb, pg = (b, 0) if g == 1 else (b - 1, 1)
                    softmax_shift(pb, pg)
                    lo(b, g, 0)
                    softmax_norm(pb, pg)
                    lo(b, g, 1)
                    raw_copy(nb, ng, 0)
                    raw_copy(nb, ng, 1)
                    cross_weights(pb, pg, 1)
                    lo(b, g, 2)
                    lo(b, g, 3)
                    raw_copy(nb, ng, 2)
                    raw_copy(nb, ng, 3)
                    if turn is not None:
                        find(turn)
                    if before_last:
                        tokens_of_slots()
                    if g == 0:
                        residual(pb)
                    cross_weights(b, g, 0)

                def last_step(b, g):
                    softmax_shift(b, 0)
                    lo(b, g, 0)
                    softmax_norm(b, 0)
                    lo(b, g, 1)
                    cross_weights(b, 0, 1)
                    lo(b, g, 2)
                    onehots(0, 0, first=True)
                    onehots(0, 1, first=True)
                    lo(b, g, 3)
                    for k in range(2):
                        onehots(1, k)
                        gathered_lo(0, k)
                    cross_weights(b, g, 0)
                    softmax_shift(b, g)
                    cross_weights(b, g, 1)
                    softmax_norm(b, g)
                    for k in range(2):
                        onehots(2, k)
                        gathered_lo(1, k)
                    slot_rows()
                    for k in range(2):
                        onehots(3, k)
                        gathered_lo(2, k)
                    for k in range(2):
                        gathered_lo(3, k)
                    residual(b)

                def done(ins):
                    ins.then_inc(early_dve, 1)

                def after(name):
                    dve.wait_ge(early_dve, dve_n[name])

                lg = DB[:, 0:NT * (H + E)].rearrange("p (t c) -> p t c", t=NT)

                def gates_and_router():
                    dve.wait_ge(early_pe, pe_n["logits"])
                    done(dve.tensor_tensor(z[:, :, :], lg[:, :, 0:H], bc(bg_in[:, :].unsqueeze(1), P, NT, H), ALU.add))
                    after("z")
                    done(dve.tensor_scalar(zn[:, :, :], z[:, :, :], -1.0, 0.0, ALU.mult, ALU.max))
                    after("zn")
                    done(dve.scalar_tensor_tensor(out=za[:, :, :], in0=zn[:, :, :], scalar=2.0, in1=z[:, :, :],
                                                  op0=ALU.mult, op1=ALU.add))
                    done(dve.tensor_reduce(gmax[:, :], lg[:, :, H:H + E], AX.X, ALU.max))
                    after("gmax")
                    done(dve.tensor_tensor(gsh[:, :, :], lg[:, :, H:H + E], bc(gmax[:, :].unsqueeze(2), P, NT, E),
                                           ALU.subtract))

                def router_probs():
                    dve.wait_ge(early_act, act_n["zln"])
                    done(dve.tensor_tensor(logg[:, :, :], za[:, :, :], zn[:, :, :], ALU.add))
                    dve.wait_ge(early_act, act_n["gexp"])
                    done(dve.reduce_sum(gsum[:, :], gsh[:, :, :], AX.X))
                    after("gsum")
                    done(dve.reciprocal(ginv[:, :], gsum[:, :]))
                    after("ginv")
                    done(dve.tensor_tensor(
                        probs[:, :, :, :].rearrange("p h b e -> p b h e"),
                        gsh[:, :, :].rearrange("p (b h) e -> p b h e", h=HT),
                        bc(ginv[:, :].rearrange("p (b h) -> p b h", h=HT).unsqueeze(3), P, B, HT, E), ALU.mult))

                def value_weights_lo():
                    for j in range(2):
                        dve.wait_ge(early_act, act_n[f"n{j}"])
                        cols = slice(j * GW, (j + 1) * GW)
                        done(dve.tensor_tensor(proj_w[:, 2, 1, cols], (XB, OB)[j][:, :],
                                               proj_w[:, 2, 0, cols].bitcast(fp32), ALU.subtract))

                def decays_and_probs():
                    dve.wait_ge(early_act, act_n["decay3"])
                    flat = decay[:, :, :, :].rearrange("p b h k -> p (b h k)")
                    done(dve.tensor_scalar(flat, flat, cross_c[:, 0:1], None, ALU.mult))
                    dve.wait_ge(early_pe, pe_n["probsT"])
                    done(dve.tensor_copy(left[:, :], XB[0:B * E, 0:T]))

                raw_copy(0, 0, 0)
                raw_copy(0, 0, 1)
                rows = ident[0:B * E, 0:B * E].rearrange("p (b e) -> p b e", b=B)
                dve.reduce_sum(emask[:, :], rows.rearrange("p b e -> p e b"), AX.X).then_inc(masks_s, 1)
                dve.reduce_sum(bmask[:, :], rows, AX.X).then_inc(masks_s, 1)
                dve.wait_ge(masks_s, 2)
                dve.tensor_copy(pick_b[:, :, :], bc(bmask[:, :].unsqueeze(2), B * E, B, P)).then_inc(masks_s, 1)
                dve.tensor_copy(tok_row[:, :], row_i[:, :]).then_inc(masks_s, 1)
                dve.tensor_copy(tok_col[:, :], col_i[:, :]).then_inc(masks_s, 1)
                dve.wait_ge(masks_s, 5)
                raw_copy(0, 0, 2)
                raw_copy(0, 0, 3)
                gates_and_router()
                router_probs()
                lo(0, 0, 0)
                lo(0, 0, 1)
                raw_copy(0, 1, 0)
                raw_copy(0, 1, 1)
                lo(0, 0, 2)
                lo(0, 0, 3)
                value_weights_lo()
                raw_copy(0, 1, 2)
                raw_copy(0, 1, 3)
                decays_and_probs()
                after("left")
                cross_weights(0, 0, 0)
                step(0, 1, turn=0)
                step(1, 0, turn=1)
                with dve.Fori(1, B - 2) as j:
                    step(j, 1, turn=j + 1)
                    step(j + 1, 0)
                step(B - 2, 1, turn=B - 1)
                step(B - 1, 0, before_last=True)
                last_step(B - 1, 1)

        with ExitStack() as c3:
            def sb3(name, shape, dt=fp32):
                return c3.enter_context(nc.sbuf_tensor(name, shape, dt))

            def sem3(name):
                return c3.enter_context(nc.semaphore(name))

            def sems3(name, n):
                return [sem3(f"{name}{i}") for i in range(n)]

            hid = [sb3(f"hid{i}", [P, FT, NSLOT]) for i in range(2)]
            back = [sb3(f"back{i}", [P, BP, 2 * T], fp32r) for i in range(2)]
            y = [sb3(f"y{i}", [P, BP, D]) for i in range(2)]
            y_hl = [sb3(f"y_hl{i}", [P, 2, BP, D], fp32r) for i in range(2)]
            moe = sb3("moe", [P, NT * P], bf16)

            up = sems3("up_done", FT)
            gelu = sems3("gelu_done", FT)
            down = sem3("down_done")
            gated = sem3("gated")
            y_hi = sem3("y_hi")
            y_lo = sem3("y_lo")
            back_s = sem3("scatter_ready")
            scat = sem3("scattered")
            moe_s = sem3("moe_rounded")
            moe_t = sem3("moe_turned")
            res_s = sem3("summed_up")
            out_s = sem3("stored")

            ACC = bank[0:4]
            UPB = [bank[4], bank[5], bank[6]]
            YB = [bank[7], bank[4]]
            block = c3.enter_context(nc.Block())
            out_v = out.rearrange("b (h p) d -> p (b h) d", p=P)

            @block.sync
            def _(sp):
                for m in range(4):
                    sp.wait_ge(res_s, m + 1)
                    sp.dma_start(out_v[:, 4 * m:4 * m + 4, :], x_in[:, 4 * m:4 * m + 4, :]).then_inc(out_s, 16)
                sp.wait_ge(out_s, 64)

            @block.tensor
            def _(pe):
                def ups(e, par, j):
                    pe.wait_ge(w1l_s[par], j + 1)
                    for f in range(FT):
                        if f == 3:
                            pe.wait_ge(gelu[0], e + 1)
                        elif not isinstance(e, int) or e:
                            pe.wait_ge(gelu[f + 1 if par else (2, 3, 1)[f]], e)
                        for n, (a_, b_) in enumerate(((1, 0), (0, 1), (0, 0))):
                            mm = pe.matmul(UPB[(f + par) % 3][:, :], w1_hl[par][:, a_, f * P:(f + 1) * P],
                                           picked[b_][:, ds(e, 1), :].rearrange("p o s -> p (o s)"),
                                           start=(n == 0), stop=(n == 2))
                        mm.then_inc(up[f], 1)

                def downs(e, par, j, last=False):
                    pe.wait_ge(gelu[FT - 1], e + 1)
                    y_bank = YB[last]
                    if (not isinstance(e, int) or e) and not last:
                        pe.wait_ge(gated, e)
                    for s in range(BP):
                        for f in range(FT):
                            mm = pe.matmul(y_bank[:, s * D:(s + 1) * D], hid[par][:, f, s * P:(s + 1) * P],
                                           w2_in[:, ds(FT * e + f, 1), :].rearrange("p o d -> p (o d)"),
                                           start=(f == 0), stop=(f == FT - 1))
                    mm.then_inc(down, 1)

                def turn_moe(m):
                    pe.wait_ge(moe_s, m + 1)
                    for t in range(4):
                        mm = pe.transpose(bank[4 + m][:, :].bitcast(bf16)[:, t * P:(t + 1) * P],
                                          moe[:, (4 * m + t) * P:(4 * m + t + 1) * P], ident_b[:, :])
                    mm.then_inc(moe_t, 1)

                def scatter(e, par, first=False, last=False):
                    pe.wait_ge(y_lo, e + 1)
                    pe.wait_ge(back_s, BP * e + BP)
                    for s in range(BP):
                        for n in (1, 0):
                            mm = pe.matmul(ACC[s][:, :], y_hl[par][:, n, s, :], back[par][:, s, :],
                                           start=(first and n == 1), stop=True, skip_group_check=True)
                        if last:
                            mm.then_inc(scat, 1)
                        if last and s == 2:
                            turn_moe(0)
                    if not last:
                        mm.then_inc(scat, 1)

                ups(0, 0, 0)
                ups(1, 1, 0)
                downs(0, 0, 0)
                ups(2, 0, 1)
                scatter(0, 0, first=True)
                downs(1, 1, 0)
                ups(3, 1, 1)
                scatter(1, 1)
                downs(2, 0, 1)
                with pe.Fori(2, E // 2) as j:
                    ups(2 * j, 0, j)
                    scatter(2 * j - 2, 0)
                    downs(2 * j - 1, 1, j - 1)
                    ups(2 * j + 1, 1, j)
                    scatter(2 * j - 1, 1)
                    downs(2 * j, 0, j)
                downs(E - 1, 1, E // 2 - 1, last=True)
                scatter(E - 2, 0)
                scatter(E - 1, 1, last=True)
                for m in range(1, 4):
                    turn_moe(m)

            @block.scalar
            def _(act):
                def gelus(j, first=False):
                    for par in range(2):
                        e = 2 * j + par
                        for f in range(FT):
                            act.wait_ge(up[f], e + 1)
                            if f == 0 and not first:
                                act.wait_ge(down, e - 1)
                            act.activation(hid[par][:, f, :], UPB[(f + par) % 3][:, :], ACT.Gelu_apprx_tanh)\
                               .then_inc(gelu[f], 1)

                gelus(0, first=True)
                with act.Fori(1, E // 2) as j:
                    gelus(j)
                for m in range(4):
                    act.wait_ge(scat, E + m)
                    act.activation(moe[:, m * 512:(m + 1) * 512], ACC[m][:, :], ACT.Copy).then_inc(moe_s, 1)

            @block.vector
            def _(dve):
                def split_w1(par, j):
                    dve.wait_ge(up[FT - 1], 2 * j + par - 1)
                    src = w1_in[:, ds(2 * j + par, 1), :].rearrange("p o f -> p (o f)")
                    dve.tensor_copy(w1_hl[par][:, 0, :], src).then_inc(w1h_s[par], 1)
                    dve.wait_ge(w1h_s[par], j + 1)
                    dve.tensor_tensor(w1_hl[par][:, 1, :], src, w1_hl[par][:, 0, :].bitcast(fp32),
                                      ALU.subtract).then_inc(w1l_s[par], 1)

                def expert(e, par, j, peel=False, last=False, bank_y=YB[0]):
                    for s in range(BP):
                        if s == 0 and not peel:
                            dve.wait_ge(scat, e - 1)
                        dve.tensor_scalar(back[par][:, s, :], tok_row[:, :],
                                          slot_tok[:, ds(e, 1), s:s + 1].rearrange("p o k -> p (o k)"), None,
                                          ALU.is_equal).then_inc(back_s, 1)
                    if not last:
                        split_w1(par, j + 1)
                    dve.wait_ge(down, e + 1)
                    dve.tensor_tensor(y[par][:, :, :], bank_y[:, :].rearrange("p (s d) -> p s d", s=BP),
                                      bc(slot_gate[:, ds(e, 1), :].rearrange("p o s -> p (o s)").unsqueeze(2), P, BP, D),
                                      ALU.mult).then_inc(gated, 1)
                    dve.wait_ge(gated, e + 1)
                    dve.tensor_copy(y_hl[par][:, 0, :, :], y[par][:, :, :]).then_inc(y_hi, 1)
                    dve.wait_ge(y_hi, e + 1)
                    dve.tensor_tensor(y_hl[par][:, 1, :, :], y[par][:, :, :], y_hl[par][:, 0, :, :].bitcast(fp32),
                                      ALU.subtract).then_inc(y_lo, 1)

                for par in range(2):
                    expert(par, par, 0, peel=True)
                with dve.Fori(1, E // 2 - 1) as j:
                    for par in range(2):
                        expert(2 * j + par, par, j)
                for par in range(2):
                    expert(E - 2 + par, par, E // 2 - 1, last=True, bank_y=YB[par])
                for m in range(4):
                    dve.wait_ge(moe_t, m + 1)
                    dve.tensor_tensor(x_in[:, 4 * m:4 * m + 4, :], x_in[:, 4 * m:4 * m + 4, :],
                                      bank[4 + m][:, :].bitcast(bf16)[:, 0:512].rearrange("p (t d) -> p t d", t=4),
                                      ALU.add).then_inc(res_s, 1)


_INS = ['L0_attn_x', 'L0_attn_Wq', 'L0_attn_Wk', 'L0_attn_Wv', 'L0_attn_Wg', 'L0_attn_bg', 'L0_attn_Wo',
        'L0_attn_qk_gain', 'L0_ffn_gate_w', 'L0_ffn_w1', 'L0_ffn_w2']
_OUTS = [((8, 256, 128), 'float32')]


def kernel(**inputs):
    import numpy as _np
    import concourse.bacc as _bacc
    from concourse import mybir as _mybir
    from concourse.bass_utils import run_bass_kernel_spmd as _run

    nc = _bacc.Bacc("TRN2", target_bir_lowering=False, num_devices=1)
    arrays, args = {}, []
    for name in _INS:
        a = _np.ascontiguousarray(inputs[name])
        if name == 'L0_attn_qk_gain':
            a = a.reshape(1)
        arrays[f"in_{name}_dram"] = a
        args.append(nc.dram_tensor(f"in_{name}_dram", a.shape, _mybir.dt.from_np(a.dtype), kind="ExternalInput").ap())
    for i, (shape, dtype) in enumerate(_OUTS):
        dt = _mybir.dt.from_np(_np.dtype(dtype))
        args.append(nc.dram_tensor(f"out_{i}_dram", shape, dt, kind="ExternalOutput").ap())
    norm_attention_and_expert_choice_ffn_kernel(nc, *args)
    r = _run(nc, [arrays], core_ids=[0])
    got = tuple(r.results[0][f"out_{i}_dram"] for i in range(len(_OUTS)))
    return got[0]
```
